# Optimizing a Trainium2 kernel written in Bass

```python
import numpy as np
import jax
import jax.numpy as jnp

def _softmax(x, axis=-1):
    return jax.nn.softmax(x, axis=axis)

def _gelu(x):
    return jax.nn.gelu(x, approximate=True)

def _silu(x):
    return jax.nn.silu(x)

def _sigmoid(x):
    return jax.nn.sigmoid(x)

def _layernorm(x, axis=-1, eps=1e-05):
    m = jnp.mean(x, axis=axis, keepdims=True)
    v = jnp.var(x, axis=axis, keepdims=True)
    return (x - m) / jnp.sqrt(v + eps)

def _scatter_add(tgt, idx, src, axis=0):
    return tgt.at[idx].add(src)

def _segment_sum(src, seg, n):
    return jax.ops.segment_sum(src, seg, n)
kernel_name = 'mk_gnn_preln_d1_gnn_r8_87a6ae'

def setup_inputs(seed: int=0):
    np.random.seed(seed)
    _w = jnp.asarray

    def _rec_inputs():
        import jax
        import jax.numpy as jnp
        _gk = jax.random.key(seed)
        x = -0.0005121 + 1.001 * jax.random.normal(jax.random.fold_in(_gk, 1), (6250, 64), jnp.float32)
        src = jax.random.randint(jax.random.fold_in(_gk, 2), (200000,), 0, 6250, jnp.int32)
        dst = jax.random.randint(jax.random.fold_in(_gk, 3), (200000,), 0, 6250, jnp.int32)
        _o = jnp.argsort(dst, stable=True)
        src = src[_o]
        dst = dst[_o]
        edge_attr_64 = -7.08334e-05 + 0.999895 * jax.random.normal(jax.random.fold_in(_gk, 11), (200000, 64), jnp.float32)
        return (x, src, dst, edge_attr_64)
    x, src, dst, edge_attr_64 = _rec_inputs()

    def _L0_gnn_setup():
        import jax, jax.numpy as jnp
        import numpy as np
        N_BONDS = 6250
        N_EDGES = 75000
        BOND_DIM = 64
        SPH_DIM = 64
        UNITS = 64
        key = jax.random.key(seed)
        k1, k2, k3, k4, k5 = jax.random.split(key, 5)
        bond_features = jax.random.normal(k1, (N_BONDS, BOND_DIM), dtype=jnp.float32)
        edges_sph_features = jax.random.normal(k2, (N_EDGES, SPH_DIM), dtype=jnp.float32)
        seg = jnp.sort(jax.random.randint(k3, (N_EDGES,), 0, N_BONDS, dtype=jnp.int32))
        nbr = jax.random.randint(k4, (N_EDGES,), 0, N_BONDS, dtype=jnp.int32)
        edges_neighbor = jnp.stack([seg, nbr], axis=1)
        kernel = jax.random.normal(k5, (BOND_DIM + SPH_DIM, UNITS), dtype=jnp.float32) * 0.05
        bias = jnp.zeros((UNITS,), dtype=jnp.float32)
        return {'bond_features': bond_features, 'edges_sph_features': edges_sph_features, 'edges_neighbor': edges_neighbor, 'kernel': kernel, 'bias': bias}
    _L0_gnn_all = _L0_gnn_setup()
    _L0_gnn_in = {k: v for k, v in _L0_gnn_all.items() if k in ('kernel', 'bias')}
    del _L0_gnn_all
    return {'x': x, 'src': src, 'dst': dst, 'edge_attr_64': edge_attr_64, 'L0_gnn_kernel': _L0_gnn_in['kernel'], 'L0_gnn_bias': _L0_gnn_in['bias']}

def reference(x, src, dst, edge_attr_64, L0_gnn_kernel, L0_gnn_bias):
    import jax
    import jax.numpy as jnp

    def _L0_gnn_ref(bond_features, edges_sph_features, edges_neighbor, kernel, bias):
        import jax, jax.numpy as jnp
        import numpy as np
        N_BONDS = 6250
        N_EDGES = 75000
        BOND_DIM = 64
        SPH_DIM = 64
        UNITS = 64
        gathered = bond_features[edges_neighbor[:, 1]]
        concated = jnp.concatenate([gathered, edges_sph_features], axis=-1)
        aggregated = jax.ops.segment_sum(concated, edges_neighbor[:, 0], num_segments=N_BONDS, indices_are_sorted=True)
        return aggregated @ kernel + bias
    edge_index_t = jnp.stack([src, dst], axis=1)
    h = jnp.maximum(_layernorm(x, axis=-1), 0.0)
    x = x + _L0_gnn_ref(h, edge_attr_64, edge_index_t, L0_gnn_kernel, L0_gnn_bias)
    return x

_drawn_inputs = setup_inputs


def setup_inputs(seed=0):
    import zlib

    import numpy as np

    out = dict(_drawn_inputs(seed))
    spreads = {'L0_gnn_bias': (0.0, 0.426)}
    factors = {}
    for name, (base, spread) in spreads.items():
        noise = np.random.default_rng([zlib.crc32(name.encode()), seed]).standard_normal(out[name].shape)
        drawn = base * np.exp(spread * noise) if base else spread * noise
        out[name] = jnp.asarray(drawn.astype(out[name].dtype))
    for name, factor in factors.items():
        out[name] = (out[name] * factor).astype(out[name].dtype)
    return out
```

```python
import concourse.bass as bass
from concourse import mybir
from contextlib import ExitStack


N_NODES, N_EDGES, F, P = 6250, 200000, 64, 128
HI = -(-N_NODES // P)
LAST = N_NODES - (HI - 1) * P
CHUNK_J = 8
CHUNK = CHUNK_J * P
CHUNKS = N_EDGES // CHUNK
REST_P = (N_EDGES - CHUNKS * CHUNK) // CHUNK_J
SPAN = 40
Z_COLS = F + SPAN
HALF_J = CHUNK_J // 2
TURNS = (CHUNKS + 1) // 2
SRC, REL, AWAY, DST = range(4)
ACC_ROWS = N_NODES + P


def gnn_kernel(nc, x, src, dst, attr, kern, bias, out):
    fp32, i32 = mybir.dt.float32, mybir.dt.int32
    ALU, ACT, AX = mybir.AluOpType, mybir.ActivationFunctionType, mybir.AxisListType
    assert CHUNKS % 2 == 1 and REST_P * CHUNK_J == N_EDGES - CHUNKS * CHUNK

    ctx = ExitStack()
    with ctx:
        def sb(name, shape, dt):
            return ctx.enter_context(nc.sbuf_tensor(name, shape, dt))

        def pb(name, shape, dt):
            return ctx.enter_context(nc.psum_tensor(name, shape, dt))

        def sem(name):
            return ctx.enter_context(nc.semaphore(name))

        xres = sb("xres", [P, HI, F], fp32)
        tab = sb("tab", [P, CHUNKS + 1, 4, CHUNK_J], fp32)
        base_row = sb("base_row", [1, CHUNKS + 1], i32)
        ident = sb("ident", [P, P], fp32)
        before = sb("before", [P, P], fp32)
        iota_span = sb("iota_span", [P, SPAN], fp32)
        spare_row = sb("spare_row", [P, 1], fp32)
        ones = sb("ones", [P, 1], fp32)
        w_h = sb("w_h", [F, F], fp32)
        bias_b = sb("bias_b", [P, F], fp32)
        cover = sb("cover", [P, 3], fp32)
        bad = sb("bad", [1, 1], i32)
        z = [sb(f"z{b}", [P, CHUNK_J, Z_COLS], fp32) for b in range(2)]
        w_rows = [sb(f"w_rows{b}", [Z_COLS, F], fp32) for b in range(2)]
        cur = [sb(f"cur{b}", [P, 4, CHUNK_J], fp32) for b in range(2)]
        same = sb("same", [P, CHUNK_J, P], fp32)
        earlier = sb("earlier", [P, CHUNK_J, P], fp32)
        dup = sb("dup", [P, CHUNK_J], fp32)
        zt = sb("zt", [Z_COLS, CHUNK_J, P], fp32)
        y = [sb(f"y{b}", [P, CHUNK_J, F], fp32) for b in range(2)]
        to_row = [sb(f"to_row{b}", [P, CHUNK_J], i32) for b in range(2)]
        acc_in = sb("acc_in", [P, CHUNK_J, HI, F], fp32)
        zeros = acc_in[:, 0, :, :]
        ln = acc_in[:, 1, :, :]
        ln_sq = acc_in[:, 2, :, :]
        hw = acc_in[:, 3, :, :]
        ht = acc_in[0:F, 4:6, :, :].rearrange("p a b c -> p (a b c)")[:, 0:HI * P]
        chunk_rows = acc_in[:, 6:8, :, :].rearrange("p a b c -> p (a b c)")
        dst_chunk = chunk_rows[:, 0:2 * CHUNK].bitcast(i32).rearrange("p (g e) -> p g e", e=CHUNK)
        src_chunk = chunk_rows[:, 2 * CHUNK:4 * CHUNK].bitcast(i32).rearrange("p (g e) -> p g e", e=CHUNK)
        chunk_f = sb("chunk_f", [P, 2, 2, CHUNK], fp32)
        base_f = sb("base_f", [P, 2], fp32)
        ln_m = sb("ln_m", [P, HI], fp32)
        ln_var = sb("ln_var", [P, HI], fp32)
        ln_rstd = sb("ln_rstd", [P, HI], fp32)

        ps_t = pb("ps_t", [P, 2, HALF_J, P], fp32)
        ps_z = pb("ps_z", [P, 2, HALF_J, P], fp32)
        ps_y = pb("ps_y", [P, 2, CHUNK_J, F], fp32)
        ps_p = pb("ps_p", [P, 2, 512], fp32)

        acc = [nc.dram_tensor(f"acc{j}", [ACC_ROWS, F], fp32, kind="Internal").ap() for j in range(CHUNK_J)]
        hw_dram = nc.dram_tensor("hw_dram", [N_NODES, F], fp32, kind="Internal").ap()

        base_b = sb("base_b", [P, CHUNKS + 1], fp32)
        in_run = chunk_f[:, :, :, :].rearrange("p a b c -> p (a b c)")[:, 0:(CHUNKS + 1) * CHUNK_J].rearrange(
            "p (c j) -> p c j", j=CHUNK_J)

        def turned_bank(i):
            t = (ps_t, ps_z)[i % 2]
            return t[:, :, :, :].rearrange("p a b c -> p (a b) c")

        def ps_y_bank(i):
            return ps_y[:, i, :, :].rearrange("p j f -> p (j f)")

        chunk_in = sem("chunk_in")
        hw_part = sem("hw_part")
        base_turned = sem("base_turned")
        step1, step2, step3 = sem("earlier_ready"), sem("dup_ready"), sem("move_ready")
        rest_clear = sem("rest_clear")
        base_in = sem("base_in")
        base_ready = sem("base_ready")
        x_clear = sem("x_clear")
        x_in = sem("x_in")
        w_in = sem("w_in")
        bias_in = sem("bias_in")
        zero_ready = sem("zero_ready")
        zeroed = [sem(f"zeroed{j}") for j in range(CHUNK_J)]
        consts = sem("consts")
        dve = sem("dve")
        ln_centred = sem("ln_centred")
        ln_squared = sem("ln_squared")
        ln_var_ready = sem("ln_var_ready")
        ln_std = sem("ln_std")
        h_ready = sem("h_ready")
        ht_ready = sem("ht_ready")
        ht_kept = sem("ht_kept")
        hw_ready = sem("hw_ready")
        hw_stored = sem("hw_stored")
        rows_ready = sem("rows_ready")
        turned = sem("turned")
        turned_kept = sem("turned_kept")
        covered = sem("covered")
        total = sem("total")
        bad_ready = sem("bad_ready")
        z_landed = [sem(f"z_landed{b}") for b in range(2)]
        w_landed = [sem(f"w_landed{b}") for b in range(2)]
        cur_ready = sem("cur_ready")
        span_ready = sem("span_ready")
        t_ready = sem("t_ready")
        m_ready = sem("m_ready")
        z_ready = sem("z_ready")
        z_kept = sem("z_kept")
        y_ready = sem("y_ready")
        y_kept = sem("y_kept")
        row_ready = sem("row_ready")
        added = [sem(f"added{j}") for j in range(CHUNK_J)]
        acc_landed = [sem(f"acc_landed{j}") for j in range(CHUNK_J)]
        out_ready = sem("out_ready")
        f_cur = sem("f_cur")
        f_idx = sem("f_idx")
        f_clamped = sem("f_clamped")
        f_inside = sem("f_inside")
        f_outside = sem("f_outside")
        f_rows = sem("f_rows")
        f_masked = sem("f_masked")
        f_t = sem("f_t")
        f_m = sem("f_m")
        f_earlier = sem("f_earlier")
        f_dup = sem("f_dup")
        f_move = sem("f_move")
        f_to = sem("f_to")
        f_y = sem("f_y")
        f_kept = sem("f_kept")
        f_added = sem("f_added")
        F_ALL = 16 * CHUNK_J
        stored = sem("stored")

        full = CHUNKS * CHUNK
        dst_c = dst[0:full].rearrange("(c e) -> c e", e=CHUNK)
        src_c = src[0:full].rearrange("(c e) -> c e", e=CHUNK)
        attr_c = attr[0:full, :].rearrange("(c p j) f -> c p j f", p=P, j=CHUNK_J)
        attr_rest = attr[full:N_EDGES, :].rearrange("(p j) f -> p j f", j=CHUNK_J)

        def blocks_of(t):
            return t[0:(HI - 1) * P, :].rearrange("(b p) f -> p b f", p=P), t[(HI - 1) * P:N_NODES, :]

        def until(eng, semaphore, value):
            if not isinstance(value, int) or value > 0:
                eng.wait_ge(semaphore, value)

        def chunks(eng, body):
            body(0, 0, P)
            body(0, 1, P)
            with eng.Fori(1, TURNS - 1) as turn:
                body(turn, 0, P)
                body(turn, 1, P)
            body(TURNS - 1, 0, P)
            body(TURNS - 1, 1, REST_P)

        def further(eng, body):
            unfit = eng.value_load(bad[0:1, 0:1], min_val=0, max_val=1)
            with eng.If(unfit > 0):
                body(0, P)
                with eng.Fori(1, CHUNKS) as c:
                    body(c, P)
                body(CHUNKS, REST_P)

        groups = ((0, P), (1, CHUNKS + 1 - P))

        block = ctx.enter_context(nc.Block())

        @block.sync
        def _(sp):
            sp.wait_ge(rest_clear, 2)
            for rows, arr, arr_c in ((src_chunk, src, src_c), (dst_chunk, dst, dst_c)):
                sp.dma_start(rows[:, 0, :], arr_c[0:P, :]).then_inc(chunk_in, 16)
                sp.dma_start(rows[0:CHUNKS - P, 1, :], arr_c[P:CHUNKS, :]).then_inc(chunk_in, 16)
                sp.dma_start(rows[CHUNKS - P:CHUNKS - P + 1, 1, 0:N_EDGES - full],
                             arr[full:N_EDGES].rearrange("(a e) -> a e", a=1)).then_inc(chunk_in, 16)
            with nc.allow_non_contiguous_dma(reason="one word per chunk"):
                sp.dma_start(base_row[0:1, 0:CHUNKS], dst_c[:, 0:1].rearrange("c a -> a c")).then_inc(base_in, 16)
            sp.dma_start(base_row[0:1, CHUNKS:CHUNKS + 1],
                         dst[full:full + 1].rearrange("(a e) -> a e", a=1)).then_inc(base_in, 16)
            for b in range(2):
                sp.dma_start(w_rows[b][0:F, :], kern[F:2 * F, :]).then_inc(w_in, 16)

            def load_attr(turn, b, n):
                c = turn * 2 + b
                until(sp, z_ready, 2 * (c - 1))
                piece = attr_rest if n == REST_P else attr_c[c, :, :, :]
                sp.dma_start(z[b][0:n, :, 0:F], piece).then_inc(z_landed[b], 16)

            def load_run(turn, b, n):
                c = turn * 2 + b
                base = sp.value_load(base_row[0:1, bass.ds(c, 1)], min_val=0, max_val=N_NODES - SPAN)
                until(sp, y_ready, c - 1)
                sp.dma_start(w_rows[b][F:Z_COLS, :], hw_dram[bass.ds(base, SPAN), :]).then_inc(w_landed[b], 16)

            def load(turn, b, n):
                load_attr(turn, b, n)
                load_run(turn, b, n)

            load_attr(0, 0, P)
            load_attr(0, 1, P)
            for j in range(CHUNK_J):
                if j == 0:
                    sp.wait_ge(zero_ready, 1)
                most = acc[j][0:HI * P, :].rearrange("(p b) f -> p b f", p=P)
                sp.dma_start(most, zeros).then_inc(zeroed[j], 16)
                sp.dma_start(acc[j][HI * P:ACC_ROWS, :], zeros[0:ACC_ROWS - HI * P, 0, :]).then_inc(zeroed[j], 16)
                if j == 0:
                    sp.wait_ge(hw_part, -(-HI // CHUNK_J))
                    most, last = blocks_of(hw_dram)
                    sp.dma_start(most, hw[:, 0:HI - 1, :]).then_inc(hw_stored, 16)
                    sp.dma_start(last, hw[0:LAST, HI - 1, :]).then_inc(hw_stored, 16)
            sp.wait_ge(base_ready, 1)
            sp.wait_ge(hw_stored, 32)
            load_run(0, 0, P)
            load_run(0, 1, P)
            with sp.Fori(1, TURNS - 1) as turn:
                load(turn, 0, P)
                load(turn, 1, P)
            load(TURNS - 1, 0, P)
            load(TURNS - 1, 1, REST_P)

            unfit = sp.value_load(bad[0:1, 0:1], min_val=0, max_val=1)
            with sp.If(unfit > 0):
                sp.wait_ge(f_added, F_ALL * (CHUNKS + 1))
            for j in range(CHUNK_J):
                sp.wait_ge(added[j], 16 * (CHUNKS + 1))
                most, last = blocks_of(acc[j])
                sp.dma_start(acc_in[:, j, 0:HI - 1, :], most).then_inc(acc_landed[j], 16)
                sp.dma_start(acc_in[0:LAST, j, HI - 1, :], last).then_inc(acc_landed[j], 16)
            most, last = blocks_of(out)
            sp.wait_ge(out_ready, 1)
            sp.dma_start(most, xres[:, 0:HI - 1, :]).then_inc(stored, 16)
            sp.dma_start(last, xres[0:LAST, HI - 1, :]).then_inc(stored, 16)
            sp.wait_ge(stored, 32)

        @block.gpsimd
        def _(pool):
            pos = dict(allow_small_or_imprecise_dtypes=True)
            nc.gpsimd.memset(src_chunk[:, 1, :], -1).then_inc(rest_clear, 1)
            nc.gpsimd.memset(dst_chunk[:, 1, :], -1).then_inc(rest_clear, 1)
            nc.gpsimd.memset(zeros, 0.0).then_inc(zero_ready, 1)
            nc.gpsimd.memset(ones[:, :], 1.0)
            nc.gpsimd.memset(before[:, :], 1.0)
            nc.gpsimd.memset(ident[:, :], 0.0).then_inc(consts, 1)
            pool.wait_ge(consts, 1)
            nc.gpsimd.affine_select(out=ident[:, :], in_=ident[:, :], pattern=[[-1, P]], base=0,
                                    channel_multiplier=1, compare_op=ALU.not_equal, fill=1.0)
            nc.gpsimd.affine_select(out=before[:, :], in_=before[:, :], pattern=[[-1, P]], base=0,
                                    channel_multiplier=1, compare_op=ALU.is_gt, fill=0.0)
            nc.gpsimd.iota(iota_span[:, :], pattern=[[1, SPAN]], base=0, channel_multiplier=0, **pos)
            nc.gpsimd.iota(spare_row[:, :], pattern=[[1, 1]], base=N_NODES, channel_multiplier=1,
                           **pos).then_inc(consts, 1)

            def add(turn, b, n):
                c = turn * 2 + b
                pool.wait_ge(row_ready, c + 1)
                pool.wait_ge(y_kept, c + 1)
                for j in range(CHUNK_J):
                    if isinstance(c, int) and c == 0:
                        pool.wait_ge(zeroed[j], 32)
                    until(pool, added[j], 16 * c)
                    pool.nop(nofuse=True)
                    nc.gpsimd.indirect_dma_start(
                        out=acc[j][:, :], out_offset=bass.IndirectOffsetOnAxis(ap=to_row[b][0:n, j:j + 1], axis=0),
                        in_=y[b][0:n, j, :], in_offset=None, compute_op=ALU.add).then_inc(added[j], 16)

            chunks(pool, add)

            def add_further(c, n):
                pool.wait_ge(f_idx, c + 1)
                pool.nop(nofuse=True)
                for j in range(CHUNK_J):
                    nc.gpsimd.indirect_dma_start(
                        out=z[0][0:n, j, 0:F], out_offset=None, in_=hw_dram,
                        in_offset=bass.IndirectOffsetOnAxis(ap=to_row[1][0:n, j:j + 1], axis=0)).then_inc(f_rows, 16)
                pool.wait_ge(f_to, c + 1)
                pool.wait_ge(f_kept, c + 1)
                pool.nop(nofuse=True)
                for j in range(CHUNK_J):
                    nc.gpsimd.indirect_dma_start(
                        out=acc[j][:, :], out_offset=bass.IndirectOffsetOnAxis(ap=to_row[0][0:n, j:j + 1], axis=0),
                        in_=y[0][0:n, j, :], in_offset=None, compute_op=ALU.add).then_inc(f_added, 16)

            further(pool, add_further)

        @block.scalar
        def _(act):
            act.wait_ge(x_clear, 1)
            most, last = blocks_of(x)
            act.dma_start(xres[:, 0:HI - 1, :], most).then_inc(x_in, 16)
            act.dma_start(xres[0:LAST, HI - 1, :], last).then_inc(x_in, 16)
            act.dma_start(w_h[:, :], kern[0:F, :]).then_inc(w_in, 16)
            act.dma_start(bias_b[:, :], bias.rearrange("(a f) -> a f", a=1).broadcast_to([P, F])).then_inc(bias_in, 16)
            act.wait_ge(ln_centred, 1)
            nc.scalar.square(ln_sq, ln).then_inc(ln_squared, 1)
            act.wait_ge(ln_var_ready, 1)
            nc.scalar.sqrt(ln_rstd[:, :], ln_var[:, :]).then_inc(ln_std, 1)
            for i, b in enumerate(range(0, HI, HALF_J)):
                n = min(HALF_J, HI - b)
                act.wait_ge(ht_ready, i + 1)
                nc.scalar.copy(ht[:, b * P:(b + n) * P], ps_p[0:F, i % 2, 0:n * P]).then_inc(ht_kept, 1)
            for i, b in enumerate(range(0, HI, CHUNK_J)):
                n = min(CHUNK_J, HI - b)
                act.wait_ge(hw_ready, i + 1)
                last = nc.scalar.copy(hw[:, b:b + n, :].rearrange("p b f -> p (b f)"), ps_y_bank(i % 2)[:, 0:n * F])
                last.then_inc(hw_part, 1)

            def keep(turn, b, n):
                c = turn * 2 + b
                for h in range(2):
                    act.wait_ge(z_ready, 2 * c + h + 1)
                    if h == 0:
                        until(act, y_ready, c)
                    nc.scalar.copy(zt[:, h * HALF_J:(h + 1) * HALF_J, 0:n],
                                   ps_z[0:Z_COLS, h, :, 0:n]).then_inc(z_kept, 1)
                act.wait_ge(y_ready, c + 1)
                for j in range(CHUNK_J):
                    until(act, added[j], 16 * (c - 1))
                nc.scalar.copy(y[b][0:n, :, :], ps_y[0:n, b, :, :]).then_inc(y_kept, 1)

            chunks(act, keep)

            def keep_further(c, n):
                act.wait_ge(f_y, c + 1)
                nc.scalar.copy(y[0][0:n, :, :], ps_y[0:n, 0, :, :]).then_inc(f_kept, 1)

            further(act, keep_further)

        @block.vector
        def _(vec):
            links = [0]

            def link(ins):
                links[0] += 1
                ins.then_inc(dve, 1)
                vec.wait_ge(dve, links[0])

            nc.vector.memset(xres[:, HI - 1, :], 0.0).then_inc(x_clear, 1)
            nc.vector.memset(cover[:, :], 0.0)
            vec.wait_ge(x_in, 32)
            link(nc.vector.tensor_reduce(ln_m[:, :], xres[:, :, :], AX.X, ALU.add))
            link(nc.vector.tensor_scalar(ln_m[:, :], ln_m[:, :], 1.0 / F, None, ALU.mult))
            nc.vector.tensor_tensor(ln, xres[:, :, :], ln_m[:, :].unsqueeze(2).broadcast_to([P, HI, F]),
                                    ALU.subtract).then_inc(ln_centred, 1)
            vec.wait_ge(ln_squared, 1)
            link(nc.vector.tensor_reduce(ln_var[:, :], ln_sq, AX.X, ALU.add))
            nc.vector.tensor_scalar(ln_var[:, :], ln_var[:, :], 1.0 / F, 1e-5, ALU.mult,
                                    ALU.add).then_inc(ln_var_ready, 1)
            vec.wait_ge(ln_std, 1)
            link(nc.vector.reciprocal(ln_rstd[:, :], ln_rstd[:, :]))
            link(nc.vector.tensor_tensor(ln, ln, ln_rstd[:, :].unsqueeze(2).broadcast_to([P, HI, F]), ALU.mult))
            nc.vector.tensor_scalar(ln, ln, 0.0, None, ALU.max).then_inc(h_ready, 1)

            vec.wait_ge(base_in, 32)
            nc.vector.tensor_scalar(base_row[:, :], base_row[:, :], float(N_NODES - SPAN), None,
                                    ALU.min).then_inc(base_ready, 1)
            vec.wait_ge(chunk_in, 96)
            link(nc.vector.tensor_scalar(base_f[:, :], dst_chunk[:, :, 0], float(N_NODES - SPAN), None, ALU.min))
            for g, n in groups:
                nc.vector.tensor_copy(chunk_f[:, 0, g, :], src_chunk[:, g, :])
                nc.vector.tensor_copy(chunk_f[:, 1, g, :], dst_chunk[:, g, :]).then_inc(rows_ready, 1)
            vec.wait_ge(consts, 2)
            for q, section in enumerate((SRC, DST)):
                for g, n in groups:
                    i = 2 * q + g
                    vec.wait_ge(turned, i + 1)
                    nc.vector.tensor_copy(tab[:, g * P:g * P + n, section, :].rearrange("p c j -> p j c"),
                                          turned_bank(i)[:, :, 0:n]).then_inc(turned_kept, 1)
            vec.wait_ge(base_turned, 1)
            vec.wait_ge(turned_kept, 4)
            link(nc.vector.tensor_copy(base_b[:, :], ps_p[:, 0, 0:CHUNKS + 1]))
            link(nc.vector.tensor_tensor(tab[:, :, REL, :], tab[:, :, DST, :],
                                         base_b[:, :].unsqueeze(2).broadcast_to([P, CHUNKS + 1, CHUNK_J]),
                                         ALU.subtract))
            link(nc.vector.tensor_scalar(tab[:, :, AWAY, :], tab[:, :, SRC, :], -1.0, spare_row[:, 0:1], ALU.mult,
                                         ALU.add))
            link(nc.vector.tensor_scalar(in_run, tab[:, :, REL, :], 0.0, SPAN - 1.0, ALU.max, ALU.min))
            link(nc.vector.tensor_tensor(in_run, in_run, tab[:, :, REL, :], ALU.is_equal))
            link(nc.vector.tensor_reduce(cover[:, 0:1], in_run[:, 0:CHUNKS, :], AX.XY, ALU.add))
            link(nc.vector.tensor_reduce(cover[0:REST_P, 1:2], in_run[0:REST_P, CHUNKS, :], AX.X, ALU.add))
            nc.vector.tensor_reduce(cover[:, 2:3], cover[:, 0:2], AX.X, ALU.add).then_inc(covered, 1)
            vec.wait_ge(total, 1)
            nc.vector.tensor_scalar(bad[0:1, 0:1], ps_p[0:1, 1, 0:1], N_EDGES - 0.5, None, ALU.is_lt).then_inc(bad_ready, 1)

            def fetch(c, b):
                nc.vector.tensor_copy(cur[b][:, :, :].rearrange("p s j -> p (s j)"),
                                      tab[:, bass.ds(c, 1), :, :].rearrange("p c s j -> p (c s j)")
                                      ).then_inc(cur_ready, 1)

            def compare(turn, b, n):
                c = turn * 2 + b
                until(vec, y_ready, c - 1)
                fetch(c, b)
                vec.wait_ge(cur_ready, c + 1)
                until(vec, z_ready, 2 * (c - 1))
                nc.vector.tensor_tensor(
                    z[b][:, :, F:Z_COLS],
                    iota_span[:, :].unsqueeze(1).broadcast_to([P, CHUNK_J, SPAN]),
                    cur[b][:, REL, :].unsqueeze(2).broadcast_to([P, CHUNK_J, SPAN]),
                    ALU.is_equal).then_inc(span_ready, 1)
                until(vec, z_ready, 2 * c)
                for h in range(2):
                    js = slice(h * HALF_J, (h + 1) * HALF_J)
                    vec.wait_ge(t_ready, 2 * c + h + 1)
                    nc.vector.tensor_tensor(same[0:n, js, 0:n], ps_t[0:n, h, :, 0:n],
                                            cur[b][0:n, SRC, js].unsqueeze(2).broadcast_to([n, HALF_J, n]),
                                            ALU.is_equal).then_inc(m_ready, 1)
                vec.wait_ge(m_ready, 2 * c + 2)
                nc.vector.tensor_tensor(earlier[0:n, :, 0:n], same[0:n, :, 0:n],
                                        before[0:n, 0:n].unsqueeze(1).broadcast_to([n, CHUNK_J, n]),
                                        ALU.mult).then_inc(step1, 1)
                vec.wait_ge(step1, c + 1)
                nc.vector.tensor_reduce(dup[0:n, :], earlier[0:n, :, 0:n], AX.X, ALU.add).then_inc(step2, 1)
                vec.wait_ge(step2, c + 1)
                nc.vector.scalar_tensor_tensor(dup[0:n, :], dup[0:n, :], 1.0, cur[b][0:n, AWAY, :], ALU.min,
                                               ALU.mult).then_inc(step3, 1)
                for j in range(CHUNK_J):
                    until(vec, added[j], 16 * (c - 1))
                vec.wait_ge(step3, c + 1)
                nc.vector.tensor_tensor(to_row[b][0:n, :], dup[0:n, :], cur[b][0:n, SRC, :],
                                        ALU.add).then_inc(row_ready, 1)

            chunks(vec, compare)

            for j in range(CHUNK_J):
                vec.wait_ge(added[j], 16 * (CHUNKS + 1))

            def compare_further(c, n):
                until(vec, f_added, F_ALL * c)
                nc.vector.tensor_copy(cur[0][:, :, :].rearrange("p s j -> p (s j)"),
                                      tab[:, bass.ds(c, 1), :, :].rearrange("p c s j -> p (c s j)")
                                      ).then_inc(f_cur, 1)
                vec.wait_ge(f_cur, c + 1)
                nc.vector.tensor_copy(to_row[1][:, :], cur[0][:, DST, :]).then_inc(f_idx, 1)
                rel, outside = cur[0][:, REL, :], cur[1][:, REL, :]
                nc.vector.tensor_scalar(outside, rel, 0.0, SPAN - 1.0, ALU.max, ALU.min).then_inc(f_clamped, 1)
                vec.wait_ge(f_clamped, c + 1)
                nc.vector.tensor_tensor(outside, outside, rel, ALU.is_equal).then_inc(f_inside, 1)
                vec.wait_ge(f_inside, c + 1)
                nc.vector.tensor_scalar(outside, outside, -1.0, 1.0, ALU.mult, ALU.add).then_inc(f_outside, 1)
                vec.wait_ge(f_outside, c + 1)
                vec.wait_ge(f_rows, F_ALL * (c + 1))
                rows = z[0][0:n, :, 0:F]
                nc.vector.tensor_tensor(rows, rows, outside[0:n, :].unsqueeze(2).broadcast_to([n, CHUNK_J, F]),
                                        ALU.mult).then_inc(f_masked, 1)
                vec.wait_ge(f_t, c + 1)
                nc.vector.tensor_tensor(
                    same[0:n, :, 0:n], ps_t[0:n, :, :, 0:n].rearrange("p h k e -> p (h k) e"),
                    cur[0][0:n, SRC, :].unsqueeze(2).broadcast_to([n, CHUNK_J, n]), ALU.is_equal).then_inc(f_m, 1)
                vec.wait_ge(f_m, c + 1)
                nc.vector.tensor_tensor(earlier[0:n, :, 0:n], same[0:n, :, 0:n],
                                        before[0:n, 0:n].unsqueeze(1).broadcast_to([n, CHUNK_J, n]),
                                        ALU.mult).then_inc(f_earlier, 1)
                vec.wait_ge(f_earlier, c + 1)
                nc.vector.tensor_reduce(dup[0:n, :], earlier[0:n, :, 0:n], AX.X, ALU.add).then_inc(f_dup, 1)
                vec.wait_ge(f_dup, c + 1)
                nc.vector.scalar_tensor_tensor(dup[0:n, :], dup[0:n, :], 1.0, cur[0][0:n, AWAY, :], ALU.min,
                                               ALU.mult).then_inc(f_move, 1)
                vec.wait_ge(f_move, c + 1)
                nc.vector.tensor_tensor(to_row[0][0:n, :], dup[0:n, :], cur[0][0:n, SRC, :],
                                        ALU.add).then_inc(f_to, 1)

            further(vec, compare_further)

            vec.wait_ge(bias_in, 16)
            link(nc.vector.tensor_tensor(xres[:, :, :], xres[:, :, :],
                                         bias_b[:, :].unsqueeze(1).broadcast_to([P, HI, F]), ALU.add))
            for j in range(CHUNK_J):
                vec.wait_ge(acc_landed[j], 32)
                most = nc.vector.tensor_tensor(xres[:, 0:HI - 1, :], xres[:, 0:HI - 1, :],
                                               acc_in[:, j, 0:HI - 1, :], ALU.add)
                last = nc.vector.tensor_tensor(xres[0:LAST, HI - 1, :], xres[0:LAST, HI - 1, :],
                                               acc_in[0:LAST, j, HI - 1, :], ALU.add)
                if j == CHUNK_J - 1:
                    last.then_inc(out_ready, 1)
                else:
                    link(last)

        @block.tensor
        def _(pe):
            pe.wait_ge(consts, 2)
            for q in range(2):
                for g, n in groups:
                    i = 2 * q + g
                    pe.wait_ge(rows_ready, g + 1)
                    until(pe, turned_kept, i - 1)
                    for j in range(CHUNK_J):
                        last = nc.tensor.transpose(
                            turned_bank(i)[:, j, 0:n],
                            chunk_f[0:n, q, g, :].rearrange("c (p j) -> c j p", j=CHUNK_J)[:, j, :], ident[0:n, 0:n])
                    last.then_inc(turned, 1)
            for g, n in groups:
                last = nc.tensor.matmul(ps_p[:, 0, g * P:g * P + n], base_f[0:n, g:g + 1].broadcast_to([n, P]),
                                        ident[0:n, 0:n], start=True, stop=True)
            last.then_inc(base_turned, 1)
            pe.wait_ge(covered, 1)
            nc.tensor.matmul(ps_p[0:1, 1, 0:1], cover[:, 2:3], ones[:, :], start=True, stop=True).then_inc(total, 1)
            pe.wait_ge(bad_ready, 1)
            pe.wait_ge(h_ready, 1)
            for i, b in enumerate(range(0, HI, HALF_J)):
                until(pe, ht_kept, i - 1)
                for k in range(min(HALF_J, HI - b)):
                    last = nc.tensor.transpose(ps_p[0:F, i % 2, k * P:(k + 1) * P], ln[:, b + k, :], ident[:, :])
                last.then_inc(ht_ready, 1)
            pe.wait_ge(w_in, 48)
            pe.wait_ge(ht_kept, -(-HI // HALF_J))
            for i, b in enumerate(range(0, HI, CHUNK_J)):
                until(pe, hw_part, i - 1)
                for k in range(min(CHUNK_J, HI - b)):
                    last = nc.tensor.matmul(ps_y_bank(i % 2)[:, k * F:(k + 1) * F], ht[:, (b + k) * P:(b + k + 1) * P],
                                            w_h[:, :], start=True, stop=True)
                last.then_inc(hw_ready, 1)
            pe.wait_ge(hw_part, -(-HI // CHUNK_J))

            def multiply(turn, b, n):
                c = turn * 2 + b
                pe.wait_ge(cur_ready, c + 1)
                for h in range(2):
                    until(pe, m_ready, 2 * c + h - 1)
                    pe.nop(nofuse=True)
                    for k in range(HALF_J):
                        j = h * HALF_J + k
                        last = nc.tensor.matmul(ps_t[0:n, h, k, 0:n], cur[b][0:n, SRC, j:j + 1].broadcast_to([n, n]),
                                                ident[0:n, 0:n], start=True, stop=True)
                    last.then_inc(t_ready, 1)
                pe.wait_ge(z_landed[b], 16 * (turn + 1))
                pe.wait_ge(span_ready, c + 1)
                for h in range(2):
                    pe.wait_ge(m_ready, 2 * c + h + 1)
                    until(pe, z_kept, 2 * c + h - 1)
                    pe.nop(nofuse=True)
                    for k in range(HALF_J):
                        j = h * HALF_J + k
                        last = nc.tensor.matmul(ps_z[0:Z_COLS, h, k, 0:n], z[b][0:n, j, :], same[0:n, j, 0:n],
                                                start=True, stop=True)
                    last.then_inc(z_ready, 1)
                pe.wait_ge(w_landed[b], 16 * (turn + 1))
                pe.wait_ge(z_kept, 2 * c + 2)
                until(pe, y_kept, c - 1)
                pe.nop(nofuse=True)
                for j in range(CHUNK_J):
                    last = nc.tensor.matmul(ps_y[0:n, b, j, :], zt[:, j, 0:n], w_rows[b][:, :], start=True, stop=True)
                last.then_inc(y_ready, 1)

            chunks(pe, multiply)

            def multiply_further(c, n):
                pe.wait_ge(f_cur, c + 1)
                pe.nop(nofuse=True)
                for j in range(CHUNK_J):
                    last = nc.tensor.matmul(ps_t[0:n, j // HALF_J, j % HALF_J, 0:n],
                                            cur[0][0:n, SRC, j:j + 1].broadcast_to([n, n]),
                                            ident[0:n, 0:n], start=True, stop=True)
                last.then_inc(f_t, 1)
                pe.wait_ge(f_m, c + 1)
                pe.wait_ge(f_masked, c + 1)
                pe.nop(nofuse=True)
                for j in range(CHUNK_J):
                    last = nc.tensor.matmul(ps_y[0:n, 0, j, :], same[0:n, j, 0:n], z[0][0:n, j, 0:F],
                                            start=True, stop=True)
                last.then_inc(f_y, 1)

            further(pe, multiply_further)


def kernel(**inputs):
    import numpy as _np
    import concourse.bacc as _bacc
    from concourse import mybir as _mybir
    from concourse.bass_utils import run_bass_kernel_spmd as _run

    names = ["x", "src", "dst", "edge_attr_64", "L0_gnn_kernel", "L0_gnn_bias"]
    nc = _bacc.Bacc("TRN2", target_bir_lowering=False, num_devices=1)
    arrays, args = {}, []
    for name in names:
        a = _np.ascontiguousarray(inputs[name])
        arrays[f"in_{name}_dram"] = a
        args.append(nc.dram_tensor(f"in_{name}_dram", a.shape, _mybir.dt.from_np(a.dtype), kind="ExternalInput").ap())
    out = nc.dram_tensor("out_dram", (N_NODES, F), _mybir.dt.float32, kind="ExternalOutput").ap()
    gnn_kernel(nc, *args, out)
    r = _run(nc, [arrays], core_ids=[0])
    return r.results[0]["out_dram"]
```

```python
import concourse.bass as bass
from concourse import mybir
from contextlib import ExitStack


N_NODES, N_EDGES, F, P = 6250, 200000, 64, 128
BLOCKS = -(-N_NODES // P)
LAST = N_NODES - (P - 1) * BLOCKS
PARTS = ((0, LAST), (LAST, BLOCKS))
CHUNK_J = 8
CHUNK = CHUNK_J * P
CHUNKS = N_EDGES // CHUNK
REST_P = (N_EDGES - CHUNKS * CHUNK) // CHUNK_J
SPAN = 40
Z_COLS = F + SPAN
HALF_J = CHUNK_J // 2
TURNS = (CHUNKS + 1) // 2
SRC, REL, AWAY, DST = range(4)
ACCS = CHUNK_J
FEW = ACCS // 2
FEW_FROM = 2 * (TURNS - 2)
HW_ROWS = P * BLOCKS
ACC_BLOCKS = -(-(N_NODES + P) // P)
ACC_ROWS = P * ACC_BLOCKS
GROUPS = -(-BLOCKS // CHUNK_J)


def gnn_kernel(nc, x, src, dst, attr, kern, bias, out):
    fp32, i32 = mybir.dt.float32, mybir.dt.int32
    ALU, ACT, AX = mybir.AluOpType, mybir.ActivationFunctionType, mybir.AxisListType
    assert CHUNKS % 2 == 1 and REST_P * CHUNK_J == N_EDGES - CHUNKS * CHUNK

    ctx = ExitStack()
    with ctx:
        def sb(name, shape, dt):
            return ctx.enter_context(nc.sbuf_tensor(name, shape, dt))

        def pb(name, shape, dt):
            return ctx.enter_context(nc.psum_tensor(name, shape, dt))

        def sem(name):
            return ctx.enter_context(nc.semaphore(name))

        xres = sb("xres", [P, BLOCKS, F], fp32)
        tab = sb("tab", [P, CHUNKS + 1, 4, CHUNK_J], fp32)
        base_row = sb("base_row", [1, CHUNKS + 1], i32)
        ident = sb("ident", [P, P], fp32)
        before = sb("before", [P, P], fp32)
        iota_span = sb("iota_span", [P, SPAN], fp32)
        spare_row = sb("spare_row", [P, 1], fp32)
        ones = sb("ones", [P, 1], fp32)
        w_h = sb("w_h", [F, F], fp32)
        bias_b = sb("bias_b", [P, F], fp32)
        cover = sb("cover", [P, 3], fp32)
        base_b = sb("base_b", [P, CHUNKS + 1], fp32)
        bad = sb("bad", [1, 1], i32)
        z = [sb(f"z{b}", [P, CHUNK_J, Z_COLS], fp32) for b in range(2)]
        w_rows = [sb(f"w_rows{b}", [Z_COLS, F], fp32) for b in range(2)]
        cur = [sb(f"cur{b}", [P, 4, CHUNK_J], fp32) for b in range(2)]
        same = sb("same", [P, CHUNK_J, P], fp32)
        earlier = sb("earlier", [P, CHUNK_J, P], fp32)
        dup = sb("dup", [P, CHUNK_J], fp32)
        zt = sb("zt", [Z_COLS, CHUNK_J, P], fp32)
        y = [sb(f"y{b}", [P, CHUNK_J, F], fp32) for b in range(2)]
        to_row = [sb(f"to_row{b}", [P, CHUNK_J], i32) for b in range(2)]
        acc_in = sb("acc_in", [P, ACCS, BLOCKS, F], fp32)
        slot_pairs = acc_in[:, :, :, :].rearrange("p (s a) b f -> p s (a b f)", a=2)
        zeros = slot_pairs[:, 0, 0:ACC_BLOCKS * F].rearrange("p (b f) -> p b f", f=F)
        ln = acc_in[:, 2, :, :]
        ln_sq = acc_in[:, 3, :, :]
        hw = acc_in[:, 3, :, :]
        ht = slot_pairs[0:F, 2, 0:BLOCKS * P]
        dst_chunk = slot_pairs[:, 3, 0:2 * CHUNK].bitcast(i32).rearrange("p (g e) -> p g e", e=CHUNK)
        src_chunk = slot_pairs[:, 3, 2 * CHUNK:4 * CHUNK].bitcast(i32).rearrange("p (g e) -> p g e", e=CHUNK)
        chunk_f = sb("chunk_f", [P, 2, 2, CHUNK], fp32)
        base_f = sb("base_f", [P, 2], fp32)
        ln_m = sb("ln_m", [P, BLOCKS], fp32)
        ln_var = sb("ln_var", [P, BLOCKS], fp32)
        ln_rstd = sb("ln_rstd", [P, BLOCKS], fp32)

        ps_t = pb("ps_t", [P, 2, HALF_J, P], fp32)
        ps_z = pb("ps_z", [P, 2, HALF_J, P], fp32)
        ps_y = pb("ps_y", [P, 2, CHUNK_J, F], fp32)
        ps_p = pb("ps_p", [P, 2, 512], fp32)

        acc = [nc.dram_tensor(f"acc{j}", [ACC_ROWS, F], fp32, kind="Internal").ap() for j in range(ACCS)]
        hw_dram = nc.dram_tensor("hw_dram", [HW_ROWS, F], fp32, kind="Internal").ap()

        in_run = chunk_f[:, :, :, :].rearrange("p a b c -> p (a b c)")[:, 0:(CHUNKS + 1) * CHUNK_J].rearrange(
            "p (c j) -> p c j", j=CHUNK_J)

        in_ps_t, in_ps_z = (t[:, :, :, :].rearrange("p a b c -> p (a b) c") for t in (ps_t, ps_z))
        in_ps_p = ps_p[:, :, :].rearrange("p a (b c) -> p (a b) c", c=P)

        def ps_y_bank(i):
            return ps_y[:, i, :, :].rearrange("p j f -> p (j f)")

        chunk_in = [sem(f"chunk_in{g}") for g in range(2)]
        rest_clear = sem("rest_clear")
        base_turned = sem("base_turned")
        base_kept = sem("base_kept")
        base_ready = sem("base_ready")
        x_clear = sem("x_clear")
        x_in = [sem(f"x_in{i}") for i in range(2)]
        w_in = sem("w_in")
        bias_in = sem("bias_in")
        zero_ready = sem("zero_ready")
        zeroed = [sem(f"zeroed{a}") for a in range(ACCS)]
        consts = sem("consts")
        dve = sem("dve")
        step1, step2, step3 = sem("earlier_ready"), sem("dup_ready"), sem("move_ready")
        ln_centred = sem("ln_centred")
        ln_squared = sem("ln_squared")
        ln_var_ready = sem("ln_var_ready")
        ln_std = sem("ln_std")
        h_ready = sem("h_ready")
        ht_ready = sem("ht_ready")
        ht_kept = sem("ht_kept")
        hw_ready = sem("hw_ready")
        hw_kept = sem("hw_kept")
        hw_stored = sem("hw_stored")
        rows_ready = sem("rows_ready")
        turned = sem("turned")
        turned_kept = sem("turned_kept")
        covered = sem("covered")
        total = sem("total")
        bad_ready = sem("bad_ready")
        z_landed = [sem(f"z_landed{b}") for b in range(2)]
        w_landed = [sem(f"w_landed{b}") for b in range(2)]
        cur_ready = sem("cur_ready")
        span_ready = sem("span_ready")
        t_ready = sem("t_ready")
        m_ready = sem("m_ready")
        z_ready = sem("z_ready")
        z_kept = sem("z_kept")
        y_ready = sem("y_ready")
        y_kept = sem("y_kept")
        row_ready = sem("row_ready")
        added = [sem(f"added{a}") for a in range(ACCS)]
        acc_landed = [[sem(f"acc_landed{a}_{i}") for i in range(2)] for a in range(ACCS)]
        out_ready = sem("out_ready")
        f_cur = sem("f_cur")
        f_idx = sem("f_idx")
        f_clamped = sem("f_clamped")
        f_inside = sem("f_inside")
        f_outside = sem("f_outside")
        f_rows = sem("f_rows")
        f_masked = sem("f_masked")
        f_t = sem("f_t")
        f_m = sem("f_m")
        f_earlier = sem("f_earlier")
        f_dup = sem("f_dup")
        f_move = sem("f_move")
        f_to = sem("f_to")
        f_y = sem("f_y")
        f_kept = sem("f_kept")
        f_added = sem("f_added")
        F_ALL = 16 * CHUNK_J
        stored = sem("stored")

        full = CHUNKS * CHUNK
        dst_c = dst[0:full].rearrange("(c e) -> c e", e=CHUNK)
        src_c = src[0:full].rearrange("(c e) -> c e", e=CHUNK)
        attr_c = attr[0:full, :].rearrange("(c p j) f -> c p j f", p=P, j=CHUNK_J)
        attr_rest = attr[full:N_EDGES, :].rearrange("(p j) f -> p j f", j=CHUNK_J)

        def rows_of(t, part):
            b0, b1 = part
            most = t[0:(P - 1) * BLOCKS, :].rearrange("(p b) f -> p b f", b=BLOCKS)[:, b0:b1, :]
            if b0 >= LAST:
                return most, None
            return most, t[(P - 1) * BLOCKS + b0:N_NODES, :].rearrange("(p b) f -> p b f", p=1)

        def adds_before(a, c):
            if not isinstance(c, int) or c <= FEW_FROM:
                return c
            return FEW_FROM + (c - FEW_FROM) * (ACCS // FEW if a < FEW else 0)

        def until(eng, semaphore, value):
            if not isinstance(value, int) or value > 0:
                eng.wait_ge(semaphore, value)

        def chunks(eng, body, between_turns=None):
            body(0, 0, P)
            body(0, 1, P)
            if between_turns:
                between_turns()
            with eng.Fori(1, TURNS - 2) as turn:
                body(turn, 0, P)
                body(turn, 1, P)
            body(TURNS - 2, 0, P)
            body(TURNS - 2, 1, P)
            body(TURNS - 1, 0, P)
            body(TURNS - 1, 1, REST_P)

        def further(eng, body):
            eng.wait_ge(bad_ready, 1)
            unfit = eng.value_load(bad[0:1, 0:1], min_val=0, max_val=1)
            with eng.If(unfit > 0):
                body(0, P)
                with eng.Fori(1, CHUNKS) as c:
                    body(c, P)
                body(CHUNKS, REST_P)

        groups = ((0, P), (1, CHUNKS + 1 - P))

        block = ctx.enter_context(nc.Block())

        @block.sync
        def _(sp):
            pairs = ((src_chunk, src, src_c), (dst_chunk, dst, dst_c))
            for rows, arr, arr_c in pairs:
                sp.dma_start(rows[:, 0, :], arr_c[0:P, :]).then_inc(chunk_in[0], 16)
            sp.wait_ge(rest_clear, 2)
            for rows, arr, arr_c in pairs:
                sp.dma_start(rows[0:CHUNKS - P, 1, :], arr_c[P:CHUNKS, :]).then_inc(chunk_in[1], 16)
                sp.dma_start(rows[CHUNKS - P:CHUNKS - P + 1, 1, 0:N_EDGES - full],
                             arr[full:N_EDGES].rearrange("(a e) -> a e", a=1)).then_inc(chunk_in[1], 16)
            for b in range(2):
                sp.dma_start(w_rows[b][0:F, :], kern[F:2 * F, :]).then_inc(w_in, 16)

            def load_attr(turn, b, n):
                c = turn * 2 + b
                until(sp, z_ready, 2 * (c - 1))
                piece = attr_rest if n == REST_P else attr_c[c, :, :, :]
                sp.dma_start(z[b][0:n, :, 0:F], piece).then_inc(z_landed[b], 16)

            def load_run(turn, b, n):
                c = turn * 2 + b
                base = sp.value_load(base_row[0:1, bass.ds(c, 1)], min_val=0, max_val=N_NODES - SPAN)
                until(sp, y_ready, c - 1)
                sp.dma_start(w_rows[b][F:Z_COLS, :], hw_dram[bass.ds(base, SPAN), :]).then_inc(w_landed[b], 16)

            def load(turn, b, n):
                load_attr(turn, b, n)
                load_run(turn, b, n)

            def zero(a):
                sp.dma_start(acc[a].rearrange("(p b) f -> p b f", p=P), zeros).then_inc(zeroed[a], 16)

            load_attr(0, 0, P)
            load_attr(0, 1, P)
            sp.wait_ge(zero_ready, 1)
            for a in range(FEW):
                zero(a)
            sp.wait_ge(hw_kept, GROUPS)
            sp.dma_start(hw_dram.rearrange("(p b) f -> p b f", p=P), hw).then_inc(hw_stored, 16)
            sp.wait_ge(base_ready, 1)
            sp.wait_ge(hw_stored, 16)
            load_run(0, 0, P)
            load_run(0, 1, P)
            for a in range(FEW, ACCS):
                zero(a)
            sp.wait_ge(base_ready, 2)
            with sp.Fori(1, TURNS - 2) as turn:
                load(turn, 0, P)
                load(turn, 1, P)
            for b in range(2):
                load(TURNS - 2, b, P)
            load(TURNS - 1, 0, P)
            load(TURNS - 1, 1, REST_P)

            def read_back(a, part, i=0):
                b0, b1 = part
                rows = acc[a][0:HW_ROWS, :].rearrange("(p b) f -> p b f", p=P)
                sp.dma_start(acc_in[:, a, b0:b1, :], rows[:, b0:b1, :]).then_inc(acc_landed[a][i], 16)

            for a in range(FEW, ACCS):
                sp.wait_ge(added[a], 16 * adds_before(a, CHUNKS + 1))
                read_back(a, (0, BLOCKS))
            sp.wait_ge(bad_ready, 1)
            unfit = sp.value_load(bad[0:1, 0:1], min_val=0, max_val=1)
            with sp.If(unfit > 0):
                sp.wait_ge(f_added, F_ALL * (CHUNKS + 1))
            for i, part in enumerate(PARTS):
                for a in range(FEW):
                    if i == 0:
                        sp.wait_ge(added[a], 16 * adds_before(a, CHUNKS + 1))
                    read_back(a, part, i)
            sp.wait_ge(stored, 16 * 3)

        @block.gpsimd
        def _(pool):
            pos = dict(allow_small_or_imprecise_dtypes=True)
            nc.gpsimd.memset(src_chunk[:, 1, :], -1).then_inc(rest_clear, 1)
            nc.gpsimd.memset(dst_chunk[:, 1, :], -1).then_inc(rest_clear, 1)
            nc.gpsimd.memset(zeros, 0.0).then_inc(zero_ready, 1)
            nc.gpsimd.memset(ones[:, :], 1.0)
            nc.gpsimd.memset(before[:, :], 1.0)
            nc.gpsimd.memset(ident[:, :], 0.0).then_inc(consts, 1)
            pool.wait_ge(consts, 1)
            nc.gpsimd.affine_select(out=ident[:, :], in_=ident[:, :], pattern=[[-1, P]], base=0,
                                    channel_multiplier=1, compare_op=ALU.not_equal, fill=1.0)
            nc.gpsimd.affine_select(out=before[:, :], in_=before[:, :], pattern=[[-1, P]], base=0,
                                    channel_multiplier=1, compare_op=ALU.is_gt, fill=0.0)
            nc.gpsimd.iota(iota_span[:, :], pattern=[[1, SPAN]], base=0, channel_multiplier=0, **pos)
            nc.gpsimd.iota(spare_row[:, :], pattern=[[1, 1]], base=N_NODES, channel_multiplier=1,
                           **pos).then_inc(consts, 1)

            def add(turn, b, n):
                c = turn * 2 + b
                pool.wait_ge(row_ready, c + 1)
                pool.wait_ge(y_kept, c + 1)
                few = isinstance(c, int) and c >= FEW_FROM
                for j in range(CHUNK_J):
                    a = j % FEW if few else j
                    if isinstance(c, int) and c == 0:
                        pool.wait_ge(zeroed[a], 16)
                    until(pool, added[a], 16 * (adds_before(a, c) + (j // FEW if few else 0)))
                    pool.nop(nofuse=True)
                    nc.gpsimd.indirect_dma_start(
                        out=acc[a][:, :], out_offset=bass.IndirectOffsetOnAxis(ap=to_row[b][0:n, j:j + 1], axis=0),
                        in_=y[b][0:n, j, :], in_offset=None, compute_op=ALU.add).then_inc(added[a], 16)

            chunks(pool, add)

            def add_further(c, n):
                pool.wait_ge(f_idx, c + 1)
                pool.nop(nofuse=True)
                for j in range(CHUNK_J):
                    nc.gpsimd.indirect_dma_start(
                        out=z[0][0:n, j, 0:F], out_offset=None, in_=hw_dram,
                        in_offset=bass.IndirectOffsetOnAxis(ap=to_row[1][0:n, j:j + 1], axis=0)).then_inc(f_rows, 16)
                pool.wait_ge(f_to, c + 1)
                pool.wait_ge(f_kept, c + 1)
                pool.nop(nofuse=True)
                for j in range(CHUNK_J):
                    if j == FEW:
                        pool.wait_ge(f_added, 16 * FEW + F_ALL * c)
                        pool.nop(nofuse=True)
                    nc.gpsimd.indirect_dma_start(
                        out=acc[j % FEW][:, :], out_offset=bass.IndirectOffsetOnAxis(ap=to_row[0][0:n, j:j + 1], axis=0),
                        in_=y[0][0:n, j, :], in_offset=None, compute_op=ALU.add).then_inc(f_added, 16)

            further(pool, add_further)

        @block.scalar
        def _(act):
            for i, (b0, b1) in enumerate(PARTS):
                most, last = rows_of(x, PARTS[i])
                if last is None:
                    act.wait_ge(x_clear, 1)
                act.dma_start(xres[0:P - 1, b0:b1, :], most).then_inc(x_in[i], 16)
                if last is not None:
                    act.dma_start(xres[P - 1:P, b0:b1, :], last).then_inc(x_in[i], 16)
            act.dma_start(w_h[:, :], kern[0:F, :]).then_inc(w_in, 16)
            act.dma_start(bias_b[:, :], bias.rearrange("(a f) -> a f", a=1).broadcast_to([P, F])).then_inc(bias_in, 16)
            for i, (b0, b1) in enumerate(PARTS):
                act.wait_ge(ln_centred, i + 1)
                nc.scalar.square(ln_sq[:, b0:b1, :], ln[:, b0:b1, :]).then_inc(ln_squared, 1)
            for i, (b0, b1) in enumerate(PARTS):
                act.wait_ge(ln_var_ready, i + 1)
                nc.scalar.sqrt(ln_rstd[:, b0:b1], ln_var[:, b0:b1]).then_inc(ln_std, 1)
            for g in range(GROUPS):
                n = min(CHUNK_J, BLOCKS - g * CHUNK_J)
                act.wait_ge(ht_ready, g + 1)
                nc.scalar.copy(ht[:, g * CHUNK_J * P:(g * CHUNK_J + n) * P].rearrange("p (b c) -> p b c", c=P),
                               (in_ps_p, in_ps_z)[g % 2][0:F, 0:n, :]).then_inc(ht_kept, 1)

            def keep(turn, b, n):
                c = turn * 2 + b
                for h in range(2):
                    act.wait_ge(z_ready, 2 * c + h + 1)
                    if h == 0:
                        until(act, y_ready, c)
                    nc.scalar.copy(zt[:, h * HALF_J:(h + 1) * HALF_J, 0:n],
                                   ps_z[0:Z_COLS, h, :, 0:n]).then_inc(z_kept, 1)
                act.wait_ge(y_ready, c + 1)
                for a in range(ACCS):
                    until(act, added[a], 16 * adds_before(a, c - 1))
                nc.scalar.copy(y[b][0:n, :, :], ps_y[0:n, b, :, :]).then_inc(y_kept, 1)

            chunks(act, keep)

            def keep_further(c, n):
                act.wait_ge(f_y, c + 1)
                nc.scalar.copy(y[0][0:n, :, :], ps_y[0:n, 0, :, :]).then_inc(f_kept, 1)

            further(act, keep_further)

            for i, (b0, b1) in enumerate(PARTS):
                most, last = rows_of(out, PARTS[i])
                act.wait_ge(out_ready, i + 1)
                act.dma_start(most, xres[0:P - 1, b0:b1, :]).then_inc(stored, 16)
                if last is not None:
                    act.dma_start(last, xres[P - 1:P, b0:b1, :]).then_inc(stored, 16)

        @block.vector
        def _(vec):
            links = [0]

            def link(ins):
                links[0] += 1
                ins.then_inc(dve, 1)
                vec.wait_ge(dve, links[0])

            nc.vector.memset(xres[:, LAST:BLOCKS, :], 0.0).then_inc(x_clear, 1)
            nc.vector.memset(cover[:, :], 0.0)

            def of_chunks(g):
                vec.wait_ge(chunk_in[g], 32 * (g + 1))
                nc.vector.tensor_scalar(base_f[:, g:g + 1], dst_chunk[:, g, 0:1], float(N_NODES - SPAN), None,
                                        ALU.min)
                nc.vector.tensor_copy(chunk_f[:, 0, g, :], src_chunk[:, g, :])
                nc.vector.tensor_copy(chunk_f[:, 1, g, :], dst_chunk[:, g, :]).then_inc(rows_ready, 1)

            def fill_tab(g, places):
                n = groups[g][1]
                cs = slice(g * P, g * P + n)
                for q, section in enumerate((SRC, DST)):
                    vec.wait_ge(turned, 2 * g + q + 1)
                    nc.vector.tensor_copy(tab[:, cs, section, :].rearrange("p c j -> p j c"),
                                          places[q][:, :, 0:n]).then_inc(turned_kept, 1)
                vec.wait_ge(base_turned, g + 1)
                nc.vector.tensor_copy(base_b[:, cs], (ps_y_bank(0), ps_p[:, 0, :])[g][:, 0:n]).then_inc(base_kept, 1)
                vec.wait_ge(base_kept, g + 1)
                vec.wait_ge(turned_kept, 2 * g + 2)
                nc.vector.tensor_copy(base_row[0:1, cs], base_b[0:1, cs]).then_inc(base_ready, 1)
                nc.vector.tensor_tensor(tab[:, cs, REL, :], tab[:, cs, DST, :],
                                        base_b[:, cs].unsqueeze(2).broadcast_to([P, n, CHUNK_J]), ALU.subtract)
                link(nc.vector.tensor_scalar(tab[:, cs, AWAY, :], tab[:, cs, SRC, :], -1.0, spare_row[:, 0:1],
                                             ALU.mult, ALU.add))

            for i, (b0, b1) in enumerate(PARTS):
                vec.wait_ge(x_in[i], 16 * (2 - i))
                last = nc.vector.tensor_reduce(ln_m[:, b0:b1], xres[:, b0:b1, :], AX.X, ALU.add)
            link(last)
            link(nc.vector.tensor_scalar(ln_m[:, :], ln_m[:, :], 1.0 / F, None, ALU.mult))
            for b0, b1 in PARTS:
                nc.vector.tensor_tensor(ln[:, b0:b1, :], xres[:, b0:b1, :],
                                        ln_m[:, b0:b1].unsqueeze(2).broadcast_to([P, b1 - b0, F]),
                                        ALU.subtract).then_inc(ln_centred, 1)
            of_chunks(0)
            for i, (b0, b1) in enumerate(PARTS):
                vec.wait_ge(ln_squared, i + 1)
                link(nc.vector.tensor_reduce(ln_var[:, b0:b1], ln_sq[:, b0:b1, :], AX.X, ALU.add))
                nc.vector.tensor_scalar(ln_var[:, b0:b1], ln_var[:, b0:b1], 1.0 / F, 1e-5, ALU.mult,
                                        ALU.add).then_inc(ln_var_ready, 1)
            of_chunks(1)
            for i, (b0, b1) in enumerate(PARTS):
                vec.wait_ge(ln_std, i + 1)
                link(nc.vector.reciprocal(ln_rstd[:, b0:b1], ln_rstd[:, b0:b1]))
                nc.vector.scalar_tensor_tensor(ln[:, b0:b1, :], ln[:, b0:b1, :], 0.0,
                                               ln_rstd[:, b0:b1].unsqueeze(2).broadcast_to([P, b1 - b0, F]),
                                               ALU.max, ALU.mult).then_inc(h_ready, 1)
            vec.wait_ge(consts, 2)
            fill_tab(0, (in_ps_t, in_ps_z))
            for g in range(GROUPS):
                n = min(CHUNK_J, BLOCKS - g * CHUNK_J)
                vec.wait_ge(hw_ready, g + 1)
                nc.vector.tensor_copy(hw[:, g * CHUNK_J:g * CHUNK_J + n, :].rearrange("p b f -> p (b f)"),
                                      ps_y_bank(g % 2)[:, 0:n * F]).then_inc(hw_kept, 1)

            def fetch(c, b):
                nc.vector.tensor_copy(cur[b][:, :, :].rearrange("p s j -> p (s j)"),
                                      tab[:, bass.ds(c, 1), :, :].rearrange("p c s j -> p (c s j)")
                                      ).then_inc(cur_ready, 1)

            def compare(turn, b, n):
                c = turn * 2 + b
                until(vec, y_ready, c - 1)
                fetch(c, b)
                vec.wait_ge(cur_ready, c + 1)
                until(vec, z_ready, 2 * (c - 1))
                nc.vector.tensor_tensor(
                    z[b][:, :, F:Z_COLS],
                    iota_span[:, :].unsqueeze(1).broadcast_to([P, CHUNK_J, SPAN]),
                    cur[b][:, REL, :].unsqueeze(2).broadcast_to([P, CHUNK_J, SPAN]),
                    ALU.is_equal).then_inc(span_ready, 1)
                until(vec, z_ready, 2 * c)
                for h in range(2):
                    js = slice(h * HALF_J, (h + 1) * HALF_J)
                    vec.wait_ge(t_ready, 2 * c + h + 1)
                    nc.vector.tensor_tensor(same[0:n, js, 0:n], ps_t[0:n, h, :, 0:n],
                                            cur[b][0:n, SRC, js].unsqueeze(2).broadcast_to([n, HALF_J, n]),
                                            ALU.is_equal).then_inc(m_ready, 1)
                vec.wait_ge(m_ready, 2 * c + 2)
                nc.vector.tensor_tensor(earlier[0:n, :, 0:n], same[0:n, :, 0:n],
                                        before[0:n, 0:n].unsqueeze(1).broadcast_to([n, CHUNK_J, n]),
                                        ALU.mult).then_inc(step1, 1)
                vec.wait_ge(step1, c + 1)
                nc.vector.tensor_reduce(dup[0:n, :], earlier[0:n, :, 0:n], AX.X, ALU.add).then_inc(step2, 1)
                vec.wait_ge(step2, c + 1)
                nc.vector.scalar_tensor_tensor(dup[0:n, :], dup[0:n, :], 1.0, cur[b][0:n, AWAY, :], ALU.min,
                                               ALU.mult).then_inc(step3, 1)
                for a in range(ACCS):
                    until(vec, added[a], 16 * adds_before(a, c - 1))
                vec.wait_ge(step3, c + 1)
                nc.vector.tensor_tensor(to_row[b][0:n, :], dup[0:n, :], cur[b][0:n, SRC, :],
                                        ALU.add).then_inc(row_ready, 1)

            def finish_tab():
                fill_tab(1, (in_ps_p, in_ps_p))
                link(nc.vector.tensor_scalar(in_run, tab[:, :, REL, :], 0.0, SPAN - 1.0, ALU.max, ALU.min))
                link(nc.vector.tensor_tensor(in_run, in_run, tab[:, :, REL, :], ALU.is_equal))
                nc.vector.tensor_reduce(cover[:, 0:1], in_run[:, 0:CHUNKS, :], AX.XY, ALU.add)
                link(nc.vector.tensor_reduce(cover[0:REST_P, 1:2], in_run[0:REST_P, CHUNKS, :], AX.X, ALU.add))
                nc.vector.tensor_reduce(cover[:, 2:3], cover[:, 0:2], AX.X, ALU.add).then_inc(covered, 1)
                vec.wait_ge(bias_in, 16)
                link(nc.vector.tensor_tensor(xres[:, :, :], xres[:, :, :],
                                             bias_b[:, :].unsqueeze(1).broadcast_to([P, BLOCKS, F]), ALU.add))

            chunks(vec, compare, finish_tab)

            vec.wait_ge(total, 1)
            nc.vector.tensor_scalar(bad[0:1, 0:1], ps_p[0:1, 1, 0:1], N_EDGES - 0.5, None,
                                    ALU.is_lt).then_inc(bad_ready, 1)

            def take_in(a, part):
                b0, b1 = part
                return nc.vector.tensor_tensor(xres[:, b0:b1, :], xres[:, b0:b1, :], acc_in[:, a, b0:b1, :], ALU.add)

            for a in range(FEW, ACCS):
                vec.wait_ge(acc_landed[a][0], 16)
                link(take_in(a, (0, BLOCKS)))

            for a in range(ACCS):
                vec.wait_ge(added[a], 16 * adds_before(a, CHUNKS + 1))

            def compare_further(c, n):
                until(vec, f_added, F_ALL * c)
                nc.vector.tensor_copy(cur[0][:, :, :].rearrange("p s j -> p (s j)"),
                                      tab[:, bass.ds(c, 1), :, :].rearrange("p c s j -> p (c s j)")
                                      ).then_inc(f_cur, 1)
                vec.wait_ge(f_cur, c + 1)
                nc.vector.tensor_copy(to_row[1][:, :], cur[0][:, DST, :]).then_inc(f_idx, 1)
                rel, outside = cur[0][:, REL, :], cur[1][:, REL, :]
                nc.vector.tensor_scalar(outside, rel, 0.0, SPAN - 1.0, ALU.max, ALU.min).then_inc(f_clamped, 1)
                vec.wait_ge(f_clamped, c + 1)
                nc.vector.tensor_tensor(outside, outside, rel, ALU.is_equal).then_inc(f_inside, 1)
                vec.wait_ge(f_inside, c + 1)
                nc.vector.tensor_scalar(outside, outside, -1.0, 1.0, ALU.mult, ALU.add).then_inc(f_outside, 1)
                vec.wait_ge(f_outside, c + 1)
                vec.wait_ge(f_rows, F_ALL * (c + 1))
                rows = z[0][0:n, :, 0:F]
                nc.vector.tensor_tensor(rows, rows, outside[0:n, :].unsqueeze(2).broadcast_to([n, CHUNK_J, F]),
                                        ALU.mult).then_inc(f_masked, 1)
                vec.wait_ge(f_t, c + 1)
                nc.vector.tensor_tensor(
                    same[0:n, :, 0:n], ps_t[0:n, :, :, 0:n].rearrange("p h k e -> p (h k) e"),
                    cur[0][0:n, SRC, :].unsqueeze(2).broadcast_to([n, CHUNK_J, n]), ALU.is_equal).then_inc(f_m, 1)
                vec.wait_ge(f_m, c + 1)
                nc.vector.tensor_tensor(earlier[0:n, :, 0:n], same[0:n, :, 0:n],
                                        before[0:n, 0:n].unsqueeze(1).broadcast_to([n, CHUNK_J, n]),
                                        ALU.mult).then_inc(f_earlier, 1)
                vec.wait_ge(f_earlier, c + 1)
                nc.vector.tensor_reduce(dup[0:n, :], earlier[0:n, :, 0:n], AX.X, ALU.add).then_inc(f_dup, 1)
                vec.wait_ge(f_dup, c + 1)
                nc.vector.scalar_tensor_tensor(dup[0:n, :], dup[0:n, :], 1.0, cur[0][0:n, AWAY, :], ALU.min,
                                               ALU.mult).then_inc(f_move, 1)
                vec.wait_ge(f_move, c + 1)
                nc.vector.tensor_tensor(to_row[0][0:n, :], dup[0:n, :], cur[0][0:n, SRC, :],
                                        ALU.add).then_inc(f_to, 1)

            further(vec, compare_further)

            for i, part in enumerate(PARTS):
                for a in range(FEW):
                    vec.wait_ge(acc_landed[a][i], 16)
                    last = take_in(a, part)
                    if a == FEW - 1:
                        last.then_inc(out_ready, 1)
                    else:
                        link(last)

        @block.tensor
        def _(pe):
            pe.wait_ge(consts, 2)

            def turn_tab(g, places):
                n = groups[g][1]
                pe.wait_ge(rows_ready, g + 1)
                for q in range(2):
                    if g == 1 and q == 1:
                        pe.wait_ge(turned_kept, 3)
                    for j in range(CHUNK_J):
                        last = nc.tensor.transpose(
                            places[q][:, j, 0:n],
                            chunk_f[0:n, q, g, :].rearrange("c (p j) -> c j p", j=CHUNK_J)[:, j, :], ident[0:n, 0:n])
                    last.then_inc(turned, 1)
                if g == 1:
                    pe.wait_ge(turned_kept, 4)
                nc.tensor.matmul((ps_y_bank(0), ps_p[:, 0, :])[g][:, 0:n], base_f[0:n, g:g + 1].broadcast_to([n, P]),
                                 ident[0:n, 0:n], start=True, stop=True).then_inc(base_turned, 1)

            turn_tab(0, (in_ps_t, in_ps_z))
            pe.wait_ge(w_in, 48)
            for g in range(GROUPS + 1):
                if g < GROUPS:
                    until(pe, ht_kept, g - 1)
                    if g == 1:
                        pe.wait_ge(turned_kept, 2)
                    for b in range(g * CHUNK_J, min((g + 1) * CHUNK_J, BLOCKS)):
                        if b in (0, LAST):
                            pe.wait_ge(h_ready, 1 if b == 0 else 2)
                        last = nc.tensor.transpose((in_ps_p, in_ps_z)[g % 2][0:F, b - g * CHUNK_J, :], ln[:, b, :],
                                                   ident[:, :])
                    last.then_inc(ht_ready, 1)
                if g > 0:
                    pe.wait_ge(ht_kept, g)
                    until(pe, hw_kept, g - 2)
                    if g == 1:
                        pe.wait_ge(base_kept, 1)
                    for b in range((g - 1) * CHUNK_J, min(g * CHUNK_J, BLOCKS)):
                        k = b - (g - 1) * CHUNK_J
                        last = nc.tensor.matmul(ps_y_bank((g - 1) % 2)[:, k * F:(k + 1) * F], ht[:, b * P:(b + 1) * P],
                                                w_h[:, :], start=True, stop=True)
                    last.then_inc(hw_ready, 1)
            pe.wait_ge(hw_kept, GROUPS)

            def multiply(turn, b, n):
                c = turn * 2 + b
                pe.wait_ge(cur_ready, c + 1)
                for h in range(2):
                    until(pe, m_ready, 2 * c + h - 1)
                    pe.nop(nofuse=True)
                    for k in range(HALF_J):
                        j = h * HALF_J + k
                        last = nc.tensor.matmul(ps_t[0:n, h, k, 0:n], cur[b][0:n, SRC, j:j + 1].broadcast_to([n, n]),
                                                ident[0:n, 0:n], start=True, stop=True)
                    last.then_inc(t_ready, 1)
                pe.wait_ge(z_landed[b], 16 * (turn + 1))
                pe.wait_ge(span_ready, c + 1)
                for h in range(2):
                    pe.wait_ge(m_ready, 2 * c + h + 1)
                    until(pe, z_kept, 2 * c + h - 1)
                    pe.nop(nofuse=True)
                    for k in range(HALF_J):
                        j = h * HALF_J + k
                        last = nc.tensor.matmul(ps_z[0:Z_COLS, h, k, 0:n], z[b][0:n, j, :], same[0:n, j, 0:n],
                                                start=True, stop=True)
                    last.then_inc(z_ready, 1)
                pe.wait_ge(w_landed[b], 16 * (turn + 1))
                pe.wait_ge(z_kept, 2 * c + 2)
                until(pe, y_kept, c - 1)
                pe.nop(nofuse=True)
                for j in range(CHUNK_J):
                    last = nc.tensor.matmul(ps_y[0:n, b, j, :], zt[:, j, 0:n], w_rows[b][:, :], start=True, stop=True)
                last.then_inc(y_ready, 1)

            chunks(pe, multiply, lambda: turn_tab(1, (in_ps_p, in_ps_p)))
            pe.wait_ge(covered, 1)
            pe.wait_ge(base_kept, 2)
            nc.tensor.matmul(ps_p[0:1, 1, 0:1], cover[:, 2:3], ones[:, :], start=True, stop=True).then_inc(total, 1)

            def multiply_further(c, n):
                pe.wait_ge(f_cur, c + 1)
                pe.nop(nofuse=True)
                for j in range(CHUNK_J):
                    last = nc.tensor.matmul(ps_t[0:n, j // HALF_J, j % HALF_J, 0:n],
                                            cur[0][0:n, SRC, j:j + 1].broadcast_to([n, n]),
                                            ident[0:n, 0:n], start=True, stop=True)
                last.then_inc(f_t, 1)
                pe.wait_ge(f_m, c + 1)
                pe.wait_ge(f_masked, c + 1)
                pe.nop(nofuse=True)
                for j in range(CHUNK_J):
                    last = nc.tensor.matmul(ps_y[0:n, 0, j, :], same[0:n, j, 0:n], z[0][0:n, j, 0:F],
                                            start=True, stop=True)
                last.then_inc(f_y, 1)

            further(pe, multiply_further)


def kernel(**inputs):
    import numpy as _np
    import concourse.bacc as _bacc
    from concourse import mybir as _mybir
    from concourse.bass_utils import run_bass_kernel_spmd as _run

    names = ["x", "src", "dst", "edge_attr_64", "L0_gnn_kernel", "L0_gnn_bias"]
    nc = _bacc.Bacc("TRN2", target_bir_lowering=False, num_devices=1)
    arrays, args = {}, []
    for name in names:
        a = _np.ascontiguousarray(inputs[name])
        arrays[f"in_{name}_dram"] = a
        args.append(nc.dram_tensor(f"in_{name}_dram", a.shape, _mybir.dt.from_np(a.dtype), kind="ExternalInput").ap())
    out = nc.dram_tensor("out_dram", (N_NODES, F), _mybir.dt.float32, kind="ExternalOutput").ap()
    gnn_kernel(nc, *args, out)
    r = _run(nc, [arrays], core_ids=[0])
    return r.results[0]["out_dram"]
```

```python
import concourse.bass as bass
from concourse import mybir
from contextlib import ExitStack


N_NODES, N_EDGES, F, P = 6250, 200000, 64, 128
BLOCKS = -(-N_NODES // P)
LAST = N_NODES - (P - 1) * BLOCKS
PARTS = ((0, LAST), (LAST, BLOCKS))
OUT_PARTS = ((0, LAST), (LAST, 44), (44, BLOCKS))
CHUNK_J = 8
CHUNK = CHUNK_J * P
CHUNKS = N_EDGES // CHUNK
REST = N_EDGES - CHUNKS * CHUNK
REST_J = 4
REST_P = REST // REST_J
SPAN = 64
Z_COLS = F + SPAN
HALF_J = CHUNK_J // 2
TURNS = (CHUNKS + 1) // 2
MID, LO = Z_COLS, 2 * Z_COLS
SRC, REL, AWAY, DST = range(4)
ACCS = CHUNK_J
FEW = ACCS // 2
FEW_ROUNDS = CHUNK_J // FEW
FEW_UNTIL = 2
FEW_FROM = 2 * (TURNS - 2)
FEW_TILES = (CHUNKS - FEW_FROM) * CHUNK_J + REST_J
HW_ROWS = P * BLOCKS
ACC_BLOCKS = -(-(N_NODES + P) // P)
ACC_ROWS = P * ACC_BLOCKS
PAIR = 2 * F
PAIRS = -(-BLOCKS // 2)
GROUP = 512 // PAIR
GROUPS = -(-PAIRS // GROUP)
STORE_AT = 5
PIECES = 8


def gnn_kernel(nc, x, src, dst, attr, kern, bias, out):
    fp32, bf16, i32 = mybir.dt.float32, mybir.dt.bfloat16, mybir.dt.int32
    ALU, AX = mybir.AluOpType, mybir.AxisListType
    assert CHUNKS % 2 == 1 and REST_P * REST_J == REST and REST_P < P and REST_J % FEW == 0

    ctx = ExitStack()
    with ctx:
        def sb(name, shape, dt):
            return ctx.enter_context(nc.sbuf_tensor(name, shape, dt))

        def pb(name, shape, dt):
            return ctx.enter_context(nc.psum_tensor(name, shape, dt))

        def sem(name):
            return ctx.enter_context(nc.semaphore(name))

        xres = sb("xres", [P, BLOCKS, F], fp32)
        tab = sb("tab", [P, CHUNKS + 1, 4, CHUNK_J], fp32)
        base_row = sb("base_row", [1, CHUNKS + 1], i32)
        base_b = sb("base_b", [P, CHUNKS + 1], fp32)
        ident = sb("ident", [P, P], fp32)
        ident_b = sb("ident_b", [P, P], bf16)
        src_parts = sb("src_parts", [TURNS, 2, 2, CHUNK_J, P], bf16)
        before = sb("before", [P, P], bf16)
        iota_span = sb("iota_span", [P, SPAN], fp32)
        spare_row = sb("spare_row", [P, 1], fp32)
        ones = sb("ones", [P, 1], fp32)
        w_h2 = sb("w_h2", [PAIR, PAIR], fp32)
        bias_b = sb("bias_b", [P, F], fp32)
        cover = sb("cover", [P, 3], fp32)
        bad = sb("bad", [1, 1], i32)
        attr_in = [sb(f"attr_in{b}", [P, CHUNK_J, F], fp32) for b in range(2)]
        z = [sb(f"z{b}", [P, CHUNK_J, 3 * Z_COLS], bf16) for b in range(2)]
        w_rows = [sb(f"w_rows{b}", [Z_COLS, F], fp32) for b in range(2)]
        cur = [sb(f"cur{b}", [P, 4, CHUNK_J], fp32) for b in range(2)]
        same = sb("same", [P, CHUNK_J, P], bf16)
        earlier = sb("earlier", [P, CHUNK_J, P], bf16)
        dup = sb("dup", [P, CHUNK_J], fp32)
        zt = sb("zt", [Z_COLS, CHUNK_J, P], fp32)
        y = [sb(f"y{b}", [P, CHUNK_J, F], fp32) for b in range(2)]
        to_row = [sb(f"to_row{b}", [P, CHUNK_J], i32) for b in range(2)]
        acc_in = sb("acc_in", [P, ACCS, BLOCKS, F], fp32)
        slot_pairs = acc_in[:, :, :, :].rearrange("p (s a) b f -> p s (a b f)", a=2)
        zeros = slot_pairs[:, 0, 0:ACC_BLOCKS * F].rearrange("p (b f) -> p b f", f=F)
        same_f = slot_pairs[:, 0, 0:CHUNK_J * P].rearrange("p (j e) -> p j e", e=P)
        ln = acc_in[:, 2, :, :]
        ln_sq = acc_in[:, 3, :, :]
        hw = acc_in[:, 3, :, :]
        ht = slot_pairs[:, 2, 0:PAIRS * P].rearrange("p (t c) -> p t c", c=P)
        dst_chunk = slot_pairs[:, 3, 0:2 * CHUNK].bitcast(i32).rearrange("p (g e) -> p g e", e=CHUNK)
        src_chunk = slot_pairs[:, 3, 2 * CHUNK:4 * CHUNK].bitcast(i32).rearrange("p (g e) -> p g e", e=CHUNK)
        chunk_f = sb("chunk_f", [P, 2, 2, CHUNK], fp32)
        base_f = sb("base_f", [P, 2], fp32)
        ln_m = sb("ln_m", [P, BLOCKS], fp32)
        ln_var = sb("ln_var", [P, BLOCKS], fp32)
        ln_rstd = sb("ln_rstd", [P, BLOCKS], fp32)

        ps_t = pb("ps_t", [P, 2, HALF_J, P], fp32)
        ps_z = pb("ps_z", [P, 2, HALF_J, P], fp32)
        ps_y = pb("ps_y", [P, 2, CHUNK_J, F], fp32)
        ps_p = pb("ps_p", [P, 2, 512], fp32)

        acc = [nc.dram_tensor(f"acc{a}", [ACC_ROWS, F], fp32, kind="Internal").ap() for a in range(ACCS)]
        hw_dram = nc.dram_tensor("hw_dram", [HW_ROWS, F], fp32, kind="Internal").ap()

        in_run = chunk_f[:, :, :, :].rearrange("p a b c -> p (a b c)")[:, 0:(CHUNKS + 1) * CHUNK_J].rearrange(
            "p (c j) -> p c j", j=CHUNK_J)

        in_ps_t, in_ps_z = (t[:, :, :, :].rearrange("p a b c -> p (a b) c") for t in (ps_t, ps_z))
        in_ps_p = ps_p[:, :, :].rearrange("p a (b c) -> p (a b) c", c=P)
        in_ps_y = ps_y[:, :, :, :].rearrange("p a (b k) f -> p (a b) (k f)", k=2)
        ps_base = ps_t[:, 0, :, :].rearrange("p a b -> p (a b)")[:, 0:2 * TURNS].rearrange("p (g t) -> p g t", g=2)

        def ps_y_bank(i):
            return ps_y[:, i, :, :].rearrange("p j f -> p (j f)")

        src_in = sem("src_in")
        dst_in = sem("dst_in")
        src_high = sem("src_high")
        src_low = sem("src_low")
        rest_clear = sem("rest_clear")
        base_turned = sem("base_turned")
        base_kept = sem("base_kept")
        base_ready = sem("base_ready")
        x_in = [sem(f"x_in{i}") for i in range(2)]
        w_in = sem("w_in")
        bias_in = sem("bias_in")
        zero_ready = sem("zero_ready")
        w_clear = sem("w_clear")
        zeroed = [sem(f"zeroed{a}") for a in range(ACCS)]
        consts = sem("consts")
        dve = sem("dve")
        step1, step2, step3 = sem("earlier_ready"), sem("dup_ready"), sem("move_ready")
        ln_centred = sem("ln_centred")
        ln_squared = sem("ln_squared")
        ln_var_ready = sem("ln_var_ready")
        ln_std = sem("ln_std")
        h_ready = sem("h_ready")
        ht_ready = sem("ht_ready")
        ht_kept = sem("ht_kept")
        hw_ready = sem("hw_ready")
        hw_kept = sem("hw_kept")
        hw_stored = sem("hw_stored")
        src_ready = [sem(f"src_ready{g}") for g in range(2)]
        dst_ready = sem("dst_ready")
        base_first = sem("base_first")
        turned = sem("turned")
        turned_kept = sem("turned_kept")
        covered = sem("covered")
        total = sem("total")
        bad_ready = sem("bad_ready")
        z_landed = [sem(f"z_landed{b}") for b in range(2)]
        w_landed = [sem(f"w_landed{b}") for b in range(2)]
        cur_ready = sem("cur_ready")
        span_ready = sem("span_ready")
        high_ready = sem("high_ready")
        rest_ready = sem("rest_ready")
        mid_ready = sem("mid_ready")
        low_ready = sem("low_ready")
        t_ready = sem("t_ready")
        m_ready = sem("m_ready")
        z_ready = sem("z_ready")
        z_kept = sem("z_kept")
        y_ready = sem("y_ready")
        y_kept = sem("y_kept")
        row_ready = sem("row_ready")
        added = [sem(f"added{a}") for a in range(ACCS)]
        acc_landed = [[sem(f"acc_landed{a}_{i}") for i in range(len(OUT_PARTS))] for a in range(ACCS)]
        out_ready = sem("out_ready")
        f_cur = sem("f_cur")
        f_idx = sem("f_idx")
        f_clamped = sem("f_clamped")
        f_inside = sem("f_inside")
        f_outside = sem("f_outside")
        f_rows = sem("f_rows")
        f_masked = sem("f_masked")
        f_t = sem("f_t")
        f_m = sem("f_m")
        f_earlier = sem("f_earlier")
        f_dup = sem("f_dup")
        f_move = sem("f_move")
        f_to = sem("f_to")
        f_y = sem("f_y")
        f_kept = sem("f_kept")
        f_added = sem("f_added")
        F_ALL = 16 * CHUNK_J
        stored = sem("stored")

        full = CHUNKS * CHUNK
        attr_c = attr[0:full, :].rearrange("(c p j) f -> c p j f", p=P, j=CHUNK_J)
        attr_rest = attr[full:N_EDGES, :].rearrange("(p j) f -> p j f", j=REST_J)

        def rows_of(t, part):
            b0, b1 = part
            most = t[0:(P - 1) * BLOCKS, :].rearrange("(p b) f -> p b f", b=BLOCKS)[:, b0:b1, :]
            if b0 >= LAST:
                return most, None
            return most, t[(P - 1) * BLOCKS + b0:N_NODES, :].rearrange("(p b) f -> p b f", p=1)

        def tiles(n):
            return REST_J if n == REST_P else CHUNK_J

        def adds_before(a, c):
            if not isinstance(c, int):
                return c + FEW_UNTIL * (FEW_ROUNDS - 1) if a < FEW else c - FEW_UNTIL
            first = min(c, FEW_UNTIL)
            middle = min(c, FEW_FROM) - first
            last = max(c - FEW_FROM, 0) * CHUNK_J if c <= CHUNKS else FEW_TILES
            return middle + (first * FEW_ROUNDS + last // FEW if a < FEW else 0)

        def until(eng, semaphore, value):
            if not isinstance(value, int) or value > 0:
                eng.wait_ge(semaphore, value)

        def chunks(eng, body, after_first=None, before_last=None):
            for turn in range(2):
                body(turn, 0, P)
                body(turn, 1, P)
                if turn == 0 and after_first:
                    after_first()
            with eng.Fori(2, TURNS - 2) as turn:
                body(turn, 0, P)
                body(turn, 1, P)
            if before_last:
                before_last()
            body(TURNS - 2, 0, P)
            body(TURNS - 2, 1, P)
            body(TURNS - 1, 0, P)
            body(TURNS - 1, 1, REST_P)

        def with_next(turn, b, step):
            if b == 0:
                step(turn, 1, REST_P if isinstance(turn, int) and turn == TURNS - 1 else P)
            elif not (isinstance(turn, int) and turn == TURNS - 1):
                step(turn + 1, 0, P)

        def further(eng, body):
            eng.wait_ge(bad_ready, 1)
            unfit = eng.value_load(bad[0:1, 0:1], min_val=0, max_val=1)
            with eng.If(unfit > 0):
                body(0, P)
                with eng.Fori(1, CHUNKS) as c:
                    body(c, P)
                body(CHUNKS, REST_P)

        turned_parts = ((0, SRC, 0, in_ps_p), (0, SRC, 1, in_ps_t), (1, DST, 0, in_ps_z), (1, DST, 1, in_ps_y))

        block = ctx.enter_context(nc.Block())

        @block.sync
        def _(sp):
            for b in range(2):
                sp.dma_start(w_rows[b][0:F, :], kern[F:2 * F, :]).then_inc(w_in, 16)
            sp.wait_ge(rest_clear, 2)
            for rows, arr, landed in ((src_chunk, src, src_in), (dst_chunk, dst, dst_in)):
                at = (TURNS - 1) * 2 * CHUNK
                sp.dma_start(rows[0:TURNS - 1, :, :],
                             arr[0:at].rearrange("(t g e) -> t g e", g=2, e=CHUNK)).then_inc(landed, 16)
                last = rows[TURNS - 1:TURNS, :, :]
                sp.dma_start(last[:, 0, :], arr[at:full].rearrange("(a e) -> a e", a=1)).then_inc(landed, 16)
                with nc.allow_non_contiguous_dma(reason="the rest, to where its tiles' edges have their places"):
                    sp.dma_start(last[:, 1, :].rearrange("a (p j) -> a p j", j=CHUNK_J)[:, 0:REST_P, 0:REST_J],
                                 arr[full:N_EDGES].rearrange("(a p j) -> a p j", a=1, j=REST_J)).then_inc(landed, 16)

            def load_attr(turn, b, n):
                c = turn * 2 + b
                until(sp, low_ready, c - 1)
                piece = attr_rest if n == REST_P else attr_c[c, :, :, :]
                sp.dma_start(attr_in[b][0:n, 0:tiles(n), :], piece).then_inc(z_landed[b], 16)

            def load_run(turn, b, n):
                c = turn * 2 + b
                base = sp.value_load(base_row[0:1, bass.ds(c, 1)], min_val=0, max_val=N_NODES - SPAN)
                until(sp, y_ready, c - 1)
                sp.dma_start(w_rows[b][F:Z_COLS, :], hw_dram[bass.ds(base, SPAN), :]).then_inc(w_landed[b], 16)

            def load(turn, b, n):
                load_attr(turn, b, n)
                load_run(turn, b, n)

            def zero(a):
                sp.dma_start(acc[a].rearrange("(p b) f -> p b f", p=P), zeros).then_inc(zeroed[a], 16)

            load_attr(0, 0, P)
            load_attr(0, 1, P)
            sp.wait_ge(zero_ready, 1)
            for a in range(FEW):
                zero(a)
            hw_blocks = hw_dram.rearrange("(p b) f -> p b f", p=P)
            at = STORE_AT * GROUP * 2
            sp.wait_ge(hw_kept, STORE_AT)
            sp.dma_start(hw_blocks[:, 0:at, :], hw[:, 0:at, :]).then_inc(hw_stored, 16)
            sp.wait_ge(hw_kept, GROUPS)
            sp.dma_start(hw_blocks[:, at:BLOCKS, :], hw[:, at:BLOCKS, :]).then_inc(hw_stored, 16)
            sp.wait_ge(base_ready, 1)
            sp.wait_ge(hw_stored, 32)
            load_run(0, 0, P)
            load_run(0, 1, P)
            pieces = [(a, k) for a in range(FEW, ACCS) for k in range(PIECES)]
            first_tiles = FEW_UNTIL * CHUNK_J

            def zero_along(t0, t1):
                for i, (a, k) in enumerate(pieces):
                    t = i * (first_tiles - FEW + 1) // len(pieces)
                    if t0 <= t < t1:
                        until(sp, added[t % FEW], 16 * (t // FEW))
                        p0, p1 = k * P // PIECES, (k + 1) * P // PIECES
                        sp.dma_start(acc[a].rearrange("(p b) f -> p b f", p=P)[p0:p1, :, :],
                                     zeros[p0:p1, :, :]).then_inc(zeroed[a], 16)

            load_attr(1, 0, P)
            zero_along(0, HALF_J)
            load_run(1, 0, P)
            zero_along(HALF_J, CHUNK_J)
            load_attr(1, 1, P)
            zero_along(CHUNK_J, CHUNK_J + HALF_J)
            load_run(1, 1, P)
            zero_along(CHUNK_J + HALF_J, first_tiles)
            with sp.Fori(2, TURNS - 2) as turn:
                load(turn, 0, P)
                load(turn, 1, P)
            for b in range(2):
                load(TURNS - 2, b, P)
            load(TURNS - 1, 0, P)
            load(TURNS - 1, 1, REST_P)

            def read_back(a, part, i=0):
                b0, b1 = part
                rows = acc[a][0:HW_ROWS, :].rearrange("(p b) f -> p b f", p=P)
                sp.dma_start(acc_in[:, a, b0:b1, :], rows[:, b0:b1, :]).then_inc(acc_landed[a][i], 16)

            for a in range(FEW, ACCS):
                sp.wait_ge(added[a], 16 * adds_before(a, CHUNKS + 1))
                for k in range(PIECES):
                    t = ((a - FEW) * PIECES + k) * FEW_TILES // ((ACCS - FEW) * PIECES)
                    sp.wait_ge(added[t % FEW], 16 * (adds_before(0, FEW_FROM) + t // FEW))
                    read_back(a, (k * BLOCKS // PIECES, (k + 1) * BLOCKS // PIECES))
            sp.wait_ge(bad_ready, 1)
            unfit = sp.value_load(bad[0:1, 0:1], min_val=0, max_val=1)
            with sp.If(unfit > 0):
                sp.wait_ge(f_added, F_ALL * CHUNKS + 16 * REST_J)
            for i, part in enumerate(OUT_PARTS):
                for a in range(FEW):
                    if i == 0:
                        sp.wait_ge(added[a], 16 * adds_before(a, CHUNKS + 1))
                    read_back(a, part, i)
            sp.wait_ge(stored, 16 * (len(OUT_PARTS) + 1))

        @block.gpsimd
        def _(pool):
            pos = dict(allow_small_or_imprecise_dtypes=True)
            nc.gpsimd.memset(w_h2[:, :], 0.0).then_inc(w_clear, 1)
            nc.gpsimd.memset(zeros, 0.0).then_inc(zero_ready, 1)
            for rows in (src_chunk, dst_chunk):
                nc.gpsimd.memset(rows[:, 1, :], -1).then_inc(rest_clear, 1)
            nc.gpsimd.memset(ones[:, :], 1.0)
            nc.gpsimd.memset(before[:, :], 1.0)
            nc.gpsimd.memset(ident[:, :], 0.0).then_inc(consts, 1)
            pool.wait_ge(consts, 1)
            nc.gpsimd.affine_select(out=ident[:, :], in_=ident[:, :], pattern=[[-1, P]], base=0,
                                    channel_multiplier=1, compare_op=ALU.not_equal, fill=1.0)
            nc.gpsimd.affine_select(out=before[:, :], in_=before[:, :], pattern=[[-1, P]], base=0,
                                    channel_multiplier=1, compare_op=ALU.is_gt, fill=0.0)
            nc.gpsimd.memset(ident_b[:, :], 0.0).then_inc(consts, 1)
            pool.wait_ge(consts, 2)
            nc.gpsimd.affine_select(out=ident_b[:, :], in_=ident_b[:, :], pattern=[[-1, P]], base=0,
                                    channel_multiplier=1, compare_op=ALU.not_equal, fill=1.0)
            nc.gpsimd.iota(iota_span[:, :], pattern=[[1, SPAN]], base=0, channel_multiplier=0, **pos)
            nc.gpsimd.iota(spare_row[:, :], pattern=[[1, 1]], base=N_NODES, channel_multiplier=1,
                           **pos).then_inc(consts, 1)

            for g in range(2):
                pool.wait_ge(src_ready[g], 1)
                by_tiles = chunk_f[0:TURNS, 0, g, :].rearrange("t (p j) -> t j p", j=CHUNK_J)
                nc.gpsimd.tensor_copy(src_parts[:, 0, g, :, :], by_tiles).then_inc(src_high, 1)
                pool.wait_ge(src_high, g + 1)
                nc.gpsimd.tensor_tensor(src_parts[:, 1, g, :, :], by_tiles, src_parts[:, 0, g, :, :],
                                        ALU.subtract).then_inc(src_low, 1)

            def add(turn, b, n):
                c = turn * 2 + b
                pool.wait_ge(row_ready, c + 1)
                pool.wait_ge(y_kept, c + 1)
                few = isinstance(c, int) and not FEW_UNTIL <= c < FEW_FROM
                for j in range(tiles(n)):
                    a = j % FEW if few else j
                    if isinstance(c, int) and c == (0 if a < FEW else FEW_UNTIL):
                        pool.wait_ge(zeroed[a], 16 if a < FEW else 16 * PIECES)
                    until(pool, added[a], 16 * (adds_before(a, c) + (j // FEW if few else 0)))
                    pool.nop(nofuse=True)
                    nc.gpsimd.indirect_dma_start(
                        out=acc[a][:, :], out_offset=bass.IndirectOffsetOnAxis(ap=to_row[b][0:n, j:j + 1], axis=0),
                        in_=y[b][0:n, j, :], in_offset=None, compute_op=ALU.add).then_inc(added[a], 16)

            chunks(pool, add)

            def add_further(c, n):
                pool.wait_ge(f_idx, c + 1)
                pool.nop(nofuse=True)
                for j in range(tiles(n)):
                    nc.gpsimd.indirect_dma_start(
                        out=attr_in[0][0:n, j, :], out_offset=None, in_=hw_dram,
                        in_offset=bass.IndirectOffsetOnAxis(ap=to_row[1][0:n, j:j + 1], axis=0)).then_inc(f_rows, 16)
                pool.wait_ge(f_to, c + 1)
                pool.wait_ge(f_kept, c + 1)
                pool.nop(nofuse=True)
                for j in range(tiles(n)):
                    if j == FEW:
                        pool.wait_ge(f_added, 16 * FEW + F_ALL * c)
                        pool.nop(nofuse=True)
                    nc.gpsimd.indirect_dma_start(
                        out=acc[j % FEW][:, :], out_offset=bass.IndirectOffsetOnAxis(ap=to_row[0][0:n, j:j + 1], axis=0),
                        in_=y[0][0:n, j, :], in_offset=None, compute_op=ALU.add).then_inc(f_added, 16)

            further(pool, add_further)

        @block.scalar
        def _(act):
            lacks = x[0:BLOCKS - LAST, :].rearrange("(p b) f -> p b f", p=1)
            for i, (b0, b1) in enumerate(PARTS):
                most, last = rows_of(x, PARTS[i])
                act.dma_start(xres[0:P - 1, b0:b1, :], most).then_inc(x_in[i], 16)
                act.dma_start(xres[P - 1:P, b0:b1, :], lacks if last is None else last).then_inc(x_in[i], 16)
            act.wait_ge(w_clear, 1)
            for d in range(2):
                act.dma_start(w_h2[d * F:(d + 1) * F, d * F:(d + 1) * F], kern[0:F, :]).then_inc(w_in, 16)
            act.dma_start(bias_b[:, :], bias.rearrange("(a f) -> a f", a=1).broadcast_to([P, F])).then_inc(bias_in, 16)
            act.wait_ge(src_in, 48)
            nc.scalar.copy(chunk_f[0:TURNS, 0, 0, :], src_chunk[0:TURNS, 0, :]).then_inc(src_ready[0], 1)
            for i, (b0, b1) in enumerate(PARTS):
                act.wait_ge(ln_centred, i + 1)
                nc.scalar.square(ln_sq[:, b0:b1, :], ln[:, b0:b1, :]).then_inc(ln_squared, 1)
            for i, (b0, b1) in enumerate(PARTS):
                act.wait_ge(ln_var_ready, i + 1)
                nc.scalar.sqrt(ln_rstd[:, b0:b1], ln_var[:, b0:b1]).then_inc(ln_std, 1)
            for i, (_, section, g, place) in enumerate(turned_parts):
                act.wait_ge(turned, i + 1)
                nc.scalar.copy(tab[:, :, section, :].rearrange("p (t g) j -> p g j t", g=2)[:, g, :, :],
                               place[:, :, 0:TURNS]).then_inc(turned_kept, 1)
            for g in range(GROUPS):
                n = min(GROUP, PAIRS - g * GROUP)
                rows = PAIR if g < GROUPS - 1 else F
                act.wait_ge(ht_ready, g + 1)
                nc.scalar.copy(ht[0:rows, g * GROUP:g * GROUP + n, :].rearrange("p t c -> p (t c)"),
                               ps_p[0:rows, g % 2, 0:n * P]).then_inc(ht_kept, 1)

            def split(turn, b, n):
                c = turn * 2 + b
                act.wait_ge(z_landed[b], 16 * (turn + 1))
                until(act, z_ready, 2 * (c - 1))
                nc.scalar.copy(z[b][0:n, :, 0:F], attr_in[b][0:n, :, :]).then_inc(high_ready, 1)
                act.wait_ge(rest_ready, c + 1)
                nc.scalar.copy(z[b][0:n, :, MID:MID + F], attr_in[b][0:n, :, :]).then_inc(mid_ready, 1)

            def keep(turn, b, n):
                c = turn * 2 + b
                for h in range(2):
                    act.wait_ge(z_ready, 2 * c + h + 1)
                    if h == 0:
                        until(act, y_ready, c)
                    nc.scalar.copy(zt[:, h * HALF_J:(h + 1) * HALF_J, 0:n],
                                   ps_z[0:Z_COLS, h, :, 0:n]).then_inc(z_kept, 1)
                with_next(turn, b, split)
                act.wait_ge(y_ready, c + 1)
                for a in range(ACCS):
                    until(act, added[a], 16 * adds_before(a, c - 1))
                nc.scalar.copy(y[b][0:n, :, :], ps_y[0:n, b, :, :]).then_inc(y_kept, 1)

            split(0, 0, P)
            chunks(act, keep)

            def keep_further(c, n):
                act.wait_ge(f_y, c + 1)
                nc.scalar.copy(y[0][0:n, :, :], ps_y[0:n, 0, :, :]).then_inc(f_kept, 1)

            further(act, keep_further)

            for i, (b0, b1) in enumerate(OUT_PARTS):
                most, last = rows_of(out, OUT_PARTS[i])
                act.wait_ge(out_ready, i + 1)
                act.dma_start(most, xres[0:P - 1, b0:b1, :]).then_inc(stored, 16)
                if last is not None:
                    act.dma_start(last, xres[P - 1:P, b0:b1, :]).then_inc(stored, 16)

        @block.vector
        def _(vec):
            links = [0]

            def link(ins):
                links[0] += 1
                ins.then_inc(dve, 1)
                vec.wait_ge(dve, links[0])

            nc.vector.memset(cover[:, :], 0.0)
            for b in range(2):
                for at in (MID, LO):
                    nc.vector.memset(z[b][:, :, at + F:at + Z_COLS], 0.0)

            for i, (b0, b1) in enumerate(PARTS):
                vec.wait_ge(x_in[i], 32)
                last = nc.vector.tensor_reduce(ln_m[:, b0:b1], xres[:, b0:b1, :], AX.X, ALU.add)
            link(last)
            link(nc.vector.tensor_scalar(ln_m[:, :], ln_m[:, :], 1.0 / F, None, ALU.mult))
            for b0, b1 in PARTS:
                nc.vector.tensor_tensor(ln[:, b0:b1, :], xres[:, b0:b1, :],
                                        ln_m[:, b0:b1].unsqueeze(2).broadcast_to([P, b1 - b0, F]),
                                        ALU.subtract).then_inc(ln_centred, 1)
            vec.wait_ge(src_in, 48)
            nc.vector.tensor_copy(chunk_f[0:TURNS, 0, 1, :], src_chunk[0:TURNS, 1, :]).then_inc(src_ready[1], 1)
            vec.wait_ge(dst_in, 48)
            nc.vector.tensor_copy(chunk_f[0:TURNS, 1, :, :], dst_chunk[0:TURNS, :, :]).then_inc(dst_ready, 1)
            for i, (b0, b1) in enumerate(PARTS):
                vec.wait_ge(ln_squared, i + 1)
                link(nc.vector.tensor_reduce(ln_var[:, b0:b1], ln_sq[:, b0:b1, :], AX.X, ALU.add))
                nc.vector.tensor_scalar(ln_var[:, b0:b1], ln_var[:, b0:b1], 1.0 / F, 1e-5, ALU.mult,
                                        ALU.add).then_inc(ln_var_ready, 1)
            nc.vector.tensor_scalar(base_f[0:TURNS, :], dst_chunk[0:TURNS, :, 0], float(N_NODES - SPAN), None,
                                    ALU.min).then_inc(base_first, 1)
            for i, (b0, b1) in enumerate(PARTS):
                vec.wait_ge(ln_std, i + 1)
                link(nc.vector.reciprocal(ln_rstd[:, b0:b1], ln_rstd[:, b0:b1]))
                nc.vector.scalar_tensor_tensor(ln[:, b0:b1, :], ln[:, b0:b1, :], 0.0,
                                               ln_rstd[:, b0:b1].unsqueeze(2).broadcast_to([P, b1 - b0, F]),
                                               ALU.max, ALU.mult).then_inc(h_ready, 1)
            vec.wait_ge(consts, 3)
            for g in range(GROUPS):
                b0, b1 = g * GROUP * 2, min((g + 1) * GROUP * 2, BLOCKS)
                vec.wait_ge(hw_ready, g + 1)
                nc.vector.tensor_copy(hw[:, b0:b1, :].rearrange("p b f -> p (b f)"),
                                      ps_y_bank(g % 2)[:, 0:(b1 - b0) * F]).then_inc(hw_kept, 1)
                if g == 0:
                    vec.wait_ge(base_turned, 1)
                    nc.vector.tensor_copy(base_b[:, :].rearrange("p (t g) -> p g t", g=2),
                                          ps_base).then_inc(base_kept, 1)
                    vec.wait_ge(base_kept, 1)
                    nc.vector.tensor_copy(base_row[:, :], base_b[0:1, :]).then_inc(base_ready, 1)
                if g == 1:
                    vec.wait_ge(turned_kept, 4)
                    nc.vector.tensor_tensor(tab[:, :, REL, :], tab[:, :, DST, :],
                                            base_b[:, :].unsqueeze(2).broadcast_to([P, CHUNKS + 1, CHUNK_J]),
                                            ALU.subtract)
                if g == 2:
                    link(nc.vector.tensor_scalar(tab[:, :, AWAY, :], tab[:, :, SRC, :], -1.0, spare_row[:, 0:1],
                                                 ALU.mult, ALU.add))

            def fetch(c, b):
                nc.vector.tensor_copy(cur[b][:, :, :].rearrange("p s j -> p (s j)"),
                                      tab[:, bass.ds(c, 1), :, :].rearrange("p c s j -> p (c s j)")
                                      ).then_inc(cur_ready, 1)

            def compare(turn, b, n):
                c = turn * 2 + b
                until(vec, y_ready, c - 1)
                fetch(c, b)
                vec.wait_ge(cur_ready, c + 1)
                until(vec, z_ready, 2 * (c - 1))
                nc.vector.tensor_tensor(
                    z[b][:, :, F:Z_COLS],
                    iota_span[:, :].unsqueeze(1).broadcast_to([P, CHUNK_J, SPAN]),
                    cur[b][:, REL, :].unsqueeze(2).broadcast_to([P, CHUNK_J, SPAN]),
                    ALU.is_equal).then_inc(span_ready, 1)
                vec.wait_ge(high_ready, c + 1)
                nc.vector.tensor_tensor(attr_in[b][0:n, :, :], attr_in[b][0:n, :, :], z[b][0:n, :, 0:F],
                                        ALU.subtract).then_inc(rest_ready, 1)
                until(vec, z_ready, 2 * c)
                for h in range(2):
                    js = slice(h * HALF_J, (h + 1) * HALF_J)
                    vec.wait_ge(t_ready, 2 * c + h + 1)
                    nc.vector.tensor_tensor(same[0:n, js, 0:n], ps_t[0:n, h, :, 0:n],
                                            cur[b][0:n, SRC, js].unsqueeze(2).broadcast_to([n, HALF_J, n]),
                                            ALU.is_equal).then_inc(m_ready, 1)
                vec.wait_ge(mid_ready, c + 1)
                nc.vector.tensor_tensor(z[b][0:n, :, LO:LO + F], attr_in[b][0:n, :, :], z[b][0:n, :, MID:MID + F],
                                        ALU.subtract).then_inc(low_ready, 1)
                vec.wait_ge(m_ready, 2 * c + 2)
                nc.vector.tensor_tensor(earlier[0:n, :, 0:n], same[0:n, :, 0:n],
                                        before[0:n, 0:n].unsqueeze(1).broadcast_to([n, CHUNK_J, n]),
                                        ALU.mult).then_inc(step1, 1)
                vec.wait_ge(step1, c + 1)
                nc.vector.tensor_reduce(dup[0:n, :], earlier[0:n, :, 0:n], AX.X, ALU.add).then_inc(step2, 1)
                vec.wait_ge(step2, c + 1)
                nc.vector.scalar_tensor_tensor(dup[0:n, :], dup[0:n, :], 1.0, cur[b][0:n, AWAY, :], ALU.min,
                                               ALU.mult).then_inc(step3, 1)
                for a in range(ACCS):
                    until(vec, added[a], 16 * adds_before(a, c - 1))
                vec.wait_ge(step3, c + 1)
                nc.vector.tensor_tensor(to_row[b][0:n, :], dup[0:n, :], cur[b][0:n, SRC, :],
                                        ALU.add).then_inc(row_ready, 1)

            def mark_inside():
                link(nc.vector.tensor_scalar(in_run, tab[:, :, REL, :], 0.0, SPAN - 1.0, ALU.max, ALU.min))
                link(nc.vector.tensor_tensor(in_run, in_run, tab[:, :, REL, :], ALU.is_equal))

            def add_bias():
                vec.wait_ge(bias_in, 16)
                link(nc.vector.tensor_tensor(xres[:, :, :], xres[:, :, :],
                                             bias_b[:, :].unsqueeze(1).broadcast_to([P, BLOCKS, F]), ALU.add))

            chunks(vec, compare, add_bias, mark_inside)

            nc.vector.tensor_reduce(cover[:, 0:1], in_run[:, 0:CHUNKS, :], AX.XY, ALU.add)
            link(nc.vector.tensor_reduce(cover[0:REST_P, 1:2], in_run[0:REST_P, CHUNKS, 0:REST_J], AX.X, ALU.add))
            nc.vector.tensor_reduce(cover[:, 2:3], cover[:, 0:2], AX.X, ALU.add).then_inc(covered, 1)

            vec.wait_ge(total, 1)
            nc.vector.tensor_scalar(bad[0:1, 0:1], ps_p[0:1, 1, 0:1], N_EDGES - 0.5, None,
                                    ALU.is_lt).then_inc(bad_ready, 1)

            def take_in(a, part):
                b0, b1 = part
                return nc.vector.tensor_tensor(xres[:, b0:b1, :], xres[:, b0:b1, :], acc_in[:, a, b0:b1, :], ALU.add)

            for a in range(FEW, ACCS):
                vec.wait_ge(acc_landed[a][0], 16 * PIECES)
                link(take_in(a, (0, BLOCKS)))

            for a in range(ACCS):
                vec.wait_ge(added[a], 16 * adds_before(a, CHUNKS + 1))

            def compare_further(c, n):
                until(vec, f_added, F_ALL * c)
                nc.vector.tensor_copy(cur[0][:, :, :].rearrange("p s j -> p (s j)"),
                                      tab[:, bass.ds(c, 1), :, :].rearrange("p c s j -> p (c s j)")
                                      ).then_inc(f_cur, 1)
                vec.wait_ge(f_cur, c + 1)
                nc.vector.tensor_copy(to_row[1][:, :], cur[0][:, DST, :]).then_inc(f_idx, 1)
                rel, outside = cur[0][:, REL, :], cur[1][:, REL, :]
                nc.vector.tensor_scalar(outside, rel, 0.0, SPAN - 1.0, ALU.max, ALU.min).then_inc(f_clamped, 1)
                vec.wait_ge(f_clamped, c + 1)
                nc.vector.tensor_tensor(outside, outside, rel, ALU.is_equal).then_inc(f_inside, 1)
                vec.wait_ge(f_inside, c + 1)
                nc.vector.tensor_scalar(outside, outside, -1.0, 1.0, ALU.mult, ALU.add).then_inc(f_outside, 1)
                vec.wait_ge(f_outside, c + 1)
                vec.wait_ge(f_rows, F_ALL * c + 16 * tiles(n))
                rows = attr_in[0][0:n, :, :]
                nc.vector.tensor_tensor(rows, rows, outside[0:n, :].unsqueeze(2).broadcast_to([n, CHUNK_J, F]),
                                        ALU.mult).then_inc(f_masked, 1)
                vec.wait_ge(f_t, c + 1)
                nc.vector.tensor_tensor(
                    same_f[0:n, :, 0:n], ps_t[0:n, :, :, 0:n].rearrange("p h k e -> p (h k) e"),
                    cur[0][0:n, SRC, :].unsqueeze(2).broadcast_to([n, CHUNK_J, n]), ALU.is_equal).then_inc(f_m, 1)
                vec.wait_ge(f_m, c + 1)
                nc.vector.tensor_tensor(earlier[0:n, :, 0:n], same_f[0:n, :, 0:n],
                                        before[0:n, 0:n].unsqueeze(1).broadcast_to([n, CHUNK_J, n]),
                                        ALU.mult).then_inc(f_earlier, 1)
                vec.wait_ge(f_earlier, c + 1)
                nc.vector.tensor_reduce(dup[0:n, :], earlier[0:n, :, 0:n], AX.X, ALU.add).then_inc(f_dup, 1)
                vec.wait_ge(f_dup, c + 1)
                nc.vector.scalar_tensor_tensor(dup[0:n, :], dup[0:n, :], 1.0, cur[0][0:n, AWAY, :], ALU.min,
                                               ALU.mult).then_inc(f_move, 1)
                vec.wait_ge(f_move, c + 1)
                nc.vector.tensor_tensor(to_row[0][0:n, :], dup[0:n, :], cur[0][0:n, SRC, :],
                                        ALU.add).then_inc(f_to, 1)

            further(vec, compare_further)

            for i, part in enumerate(OUT_PARTS):
                for a in range(FEW):
                    vec.wait_ge(acc_landed[a][i], 16)
                    last = take_in(a, part)
                    if a == FEW - 1:
                        last.then_inc(out_ready, 1)
                    else:
                        link(last)

        @block.tensor
        def _(pe):
            pe.wait_ge(consts, 3)

            for q, _, g, place in turned_parts:
                if q == 0:
                    pe.wait_ge(src_ready[g], 1)
                else:
                    pe.wait_ge(dst_ready, 1)
                for j in range(CHUNK_J):
                    last = nc.tensor.transpose(
                        place[:, j, 0:TURNS],
                        chunk_f[0:TURNS, q, g, :].rearrange("t (p j) -> t j p", j=CHUNK_J)[:, j, :],
                        ident[0:TURNS, 0:TURNS])
                last.then_inc(turned, 1)
            pe.wait_ge(turned_kept, 2)
            pe.wait_ge(base_first, 1)
            for g in range(2):
                last = nc.tensor.matmul(ps_base[:, g, :], base_f[0:TURNS, g:g + 1].broadcast_to([TURNS, P]),
                                        ident[0:TURNS, 0:TURNS], start=True, stop=True)
            last.then_inc(base_turned, 1)
            for g in range(GROUPS + 1):
                if g < GROUPS:
                    until(pe, ht_kept, g - 1)
                    for t in range(g * GROUP, min((g + 1) * GROUP, PAIRS)):
                        if t in (0, LAST // 2):
                            pe.wait_ge(h_ready, 1 if t == 0 else 2)
                        pair = ln[:, 2 * t:min(2 * t + 2, BLOCKS), :].rearrange("p b f -> p (b f)")
                        last = nc.tensor.transpose(ps_p[0:pair.shape[1], g % 2, (t - g * GROUP) * P:][:, 0:P], pair,
                                                   ident[:, :])
                    last.then_inc(ht_ready, 1)
                if g > 0:
                    pe.wait_ge(ht_kept, g)
                    if g == 1:
                        pe.wait_ge(w_in, 64)
                        pe.wait_ge(turned_kept, 4)
                    until(pe, hw_kept, g - 2)
                    for t in range((g - 1) * GROUP, min(g * GROUP, PAIRS)):
                        k = t - (g - 1) * GROUP
                        n = PAIR if 2 * t + 2 <= BLOCKS else F
                        last = nc.tensor.matmul(ps_y_bank((g - 1) % 2)[:, k * PAIR:k * PAIR + n], ht[0:n, t, :],
                                                w_h2[0:n, 0:n], start=True, stop=True)
                    last.then_inc(hw_ready, 1)
            pe.wait_ge(hw_kept, GROUPS)
            pe.wait_ge(base_kept, 1)
            pe.wait_ge(src_low, 2)

            def spread(turn, b, n):
                c = turn * 2 + b
                pick = ident_b[0:TURNS, bass.ds(turn, 1)].broadcast_to([TURNS, P])
                for h in range(2):
                    until(pe, m_ready, 2 * c + h - 1)
                    pe.nop(nofuse=True)
                    for part in range(2):
                        last = nc.tensor.matmul(
                            ps_t[:, h, :, :].rearrange("p k e -> p (k e)"), pick,
                            src_parts[:, part, b, h * HALF_J:(h + 1) * HALF_J, :].rearrange("t k e -> t (k e)"),
                            start=part == 0, stop=part == 1)
                    last.then_inc(t_ready, 1)

            def multiply(turn, b, n):
                c = turn * 2 + b
                pe.wait_ge(span_ready, c + 1)
                pe.wait_ge(low_ready, c + 1)
                for h in range(2):
                    pe.wait_ge(m_ready, 2 * c + h + 1)
                    until(pe, z_kept, 2 * c + h - 1)
                    pe.nop(nofuse=True)
                    for k in range(HALF_J):
                        j = h * HALF_J + k
                        for at in (0, MID, LO):
                            last = nc.tensor.matmul(ps_z[0:Z_COLS, h, k, 0:n], z[b][0:n, j, at:at + Z_COLS],
                                                    same[0:n, j, 0:n], start=at == 0, stop=at == LO)
                    last.then_inc(z_ready, 1)
                with_next(turn, b, spread)
                pe.wait_ge(w_landed[b], 16 * (turn + 1))
                pe.wait_ge(z_kept, 2 * c + 2)
                until(pe, y_kept, c - 1)
                pe.nop(nofuse=True)
                for j in range(CHUNK_J):
                    last = nc.tensor.matmul(ps_y[0:n, b, j, :], zt[:, j, 0:n], w_rows[b][:, :], start=True, stop=True)
                last.then_inc(y_ready, 1)

            spread(0, 0, P)
            chunks(pe, multiply)
            pe.wait_ge(covered, 1)
            nc.tensor.matmul(ps_p[0:1, 1, 0:1], cover[:, 2:3], ones[:, :], start=True, stop=True).then_inc(total, 1)

            def multiply_further(c, n):
                pe.wait_ge(f_cur, c + 1)
                pe.nop(nofuse=True)
                for j in range(CHUNK_J):
                    last = nc.tensor.matmul(ps_t[0:n, j // HALF_J, j % HALF_J, 0:n],
                                            cur[0][0:n, SRC, j:j + 1].broadcast_to([n, n]),
                                            ident[0:n, 0:n], start=True, stop=True)
                last.then_inc(f_t, 1)
                pe.wait_ge(f_m, c + 1)
                pe.wait_ge(f_masked, c + 1)
                pe.nop(nofuse=True)
                for j in range(CHUNK_J):
                    last = nc.tensor.matmul(ps_y[0:n, 0, j, :], same_f[0:n, j, 0:n], attr_in[0][0:n, j, :],
                                            start=True, stop=True)
                last.then_inc(f_y, 1)

            further(pe, multiply_further)


def kernel(**inputs):
    import numpy as _np
    import concourse.bacc as _bacc
    from concourse import mybir as _mybir
    from concourse.bass_utils import run_bass_kernel_spmd as _run

    names = ["x", "src", "dst", "edge_attr_64", "L0_gnn_kernel", "L0_gnn_bias"]
    nc = _bacc.Bacc("TRN2", target_bir_lowering=False, num_devices=1)
    arrays, args = {}, []
    for name in names:
        a = _np.ascontiguousarray(inputs[name])
        arrays[f"in_{name}_dram"] = a
        args.append(nc.dram_tensor(f"in_{name}_dram", a.shape, _mybir.dt.from_np(a.dtype), kind="ExternalInput").ap())
    out = nc.dram_tensor("out_dram", (N_NODES, F), _mybir.dt.float32, kind="ExternalOutput").ap()
    gnn_kernel(nc, *args, out)
    r = _run(nc, [arrays], core_ids=[0])
    return r.results[0]["out_dram"]
```
